# Optimizing a Trainium2 kernel written in Bass

```python
import numpy as np
import jax
import jax.numpy as jnp

def _softmax(x, axis=-1):
    return jax.nn.softmax(x, axis=axis)

def _gelu(x):
    return jax.nn.gelu(x, approximate=True)

def _silu(x):
    return jax.nn.silu(x)

def _sigmoid(x):
    return jax.nn.sigmoid(x)

def _layernorm(x, axis=-1, eps=1e-05):
    m = jnp.mean(x, axis=axis, keepdims=True)
    v = jnp.var(x, axis=axis, keepdims=True)
    return (x - m) / jnp.sqrt(v + eps)

def _scatter_add(tgt, idx, src, axis=0):
    return tgt.at[idx].add(src)

def _segment_sum(src, seg, n):
    return jax.ops.segment_sum(src, seg, n)
kernel_name = 'mk_adj_ffn_d2_adj_r2_b25ad5'

def setup_inputs(seed: int=0):
    np.random.seed(seed)
    _w = jnp.asarray

    def _rec_inputs():
        import jax
        import jax.numpy as jnp
        _gk = jax.random.key(seed)
        x = -0.0005207 + 1.001 * jax.random.normal(jax.random.fold_in(_gk, 1), (4096, 128), jnp.float32)
        _a = jax.random.bernoulli(jax.random.fold_in(_gk, 2), 0.00390625, (4096, 4096))
        _a = jnp.logical_or(_a, jnp.swapaxes(_a, -1, -2))
        _a = jnp.logical_or(_a, jnp.eye(4096, dtype=bool))
        _af = _a.astype(jnp.float32)
        _af = _af * jax.random.uniform(jax.random.fold_in(_gk, 3), (4096, 4096), jnp.float32, 0.05, 1)
        adj = _af
        return (x, adj)
    x, adj = _rec_inputs()

    def _L0_gnn_setup():
        import jax, jax.numpy as jnp
        import numpy as np
        N, IN_DIM, HID = (4096, 128, 128)

        def _gcn_layer(x, adj, W, b):
            d_inv_sqrt = (jnp.sum(adj, axis=1) + 1e-09) ** (-0.5)
            msg = d_inv_sqrt[:, None] * adj * d_inv_sqrt[None, :] @ x
            return jax.nn.relu(msg @ W + b)
        key = jax.random.key(seed)
        ks = jax.random.split(key, 9)
        feature_x = jax.random.normal(ks[0], (N, IN_DIM), dtype=jnp.float32)
        spatial_x = jax.random.normal(ks[1], (N, IN_DIM), dtype=jnp.float32)
        adj = jax.random.uniform(ks[2], (N, N), dtype=jnp.float32)
        s_in = 1.0 / np.sqrt(IN_DIM)
        s_hid = 1.0 / np.sqrt(2 * HID)
        W_f = jax.random.uniform(ks[3], (IN_DIM, HID), dtype=jnp.float32, minval=-s_in, maxval=s_in)
        b_f = jax.random.uniform(ks[4], (HID,), dtype=jnp.float32, minval=-s_in, maxval=s_in)
        W_s = jax.random.uniform(ks[5], (IN_DIM, HID), dtype=jnp.float32, minval=-s_in, maxval=s_in)
        b_s = jax.random.uniform(ks[6], (HID,), dtype=jnp.float32, minval=-s_in, maxval=s_in)
        W_att = jax.random.uniform(ks[7], (2 * HID, 1), dtype=jnp.float32, minval=-s_hid, maxval=s_hid)
        b_att = jax.random.uniform(ks[8], (1,), dtype=jnp.float32, minval=-s_hid, maxval=s_hid)
        return {'feature_x': feature_x, 'spatial_x': spatial_x, 'adj': adj, 'W_f': W_f, 'b_f': b_f, 'W_s': W_s, 'b_s': b_s, 'W_att': W_att, 'b_att': b_att}
    _L0_gnn_all = _L0_gnn_setup()
    _L0_gnn_in = {k: v for k, v in _L0_gnn_all.items() if k in ('spatial_x', 'W_f', 'b_f', 'W_s', 'b_s', 'W_att', 'b_att')}
    del _L0_gnn_all

    def _L0_ffn_setup():
        import jax, jax.numpy as jnp
        import numpy as np
        from jax import lax
        key = jax.random.key(seed)
        B, T, I, H = (64, 1024, 128, 128)
        ks = jax.random.split(key, 13)
        s = 1.0 / np.sqrt(H)

        def w(k, shape):
            return jax.random.uniform(k, shape, jnp.float32, -s, s)
        return {'x': jax.random.normal(ks[0], (B, T, I), jnp.float32), 'U_i': w(ks[1], (I, H)), 'V_i': w(ks[2], (H, H)), 'b_i': w(ks[3], (H,)), 'U_f': w(ks[4], (I, H)), 'V_f': w(ks[5], (H, H)), 'b_f': w(ks[6], (H,)), 'U_c': w(ks[7], (I, H)), 'V_c': w(ks[8], (H, H)), 'b_c': w(ks[9], (H,)), 'U_o': w(ks[10], (I, H)), 'V_o': w(ks[11], (H, H)), 'b_o': w(ks[12], (H,))}
    _L0_ffn_all = _L0_ffn_setup()
    _L0_ffn_in = {k: v for k, v in _L0_ffn_all.items() if k in ('U_i', 'V_i', 'b_i', 'U_f', 'V_f', 'b_f', 'U_c', 'V_c', 'b_c', 'U_o', 'V_o', 'b_o')}
    del _L0_ffn_all

    def _L1_gnn_setup():
        import jax, jax.numpy as jnp
        import numpy as np
        N = 4096
        DIM = 128
        HEADS = 4
        HD = DIM // HEADS
        SCALE = HD ** (-0.5)
        key = jax.random.key(seed)
        ks = jax.random.split(key, 8)
        x = jax.random.normal(ks[0], (N, DIM), dtype=jnp.float32)
        adj_matrix = jax.random.uniform(ks[1], (N, N), dtype=jnp.float32)
        attn_mask = jax.random.randint(ks[2], (N, N), 0, 2, dtype=jnp.int32)
        Wqkv = jax.random.normal(ks[3], (DIM, 3 * DIM), dtype=jnp.float32) * DIM ** (-0.5)
        bqkv = jnp.zeros((3 * DIM,), dtype=jnp.float32)
        Wout = jax.random.normal(ks[4], (DIM, DIM), dtype=jnp.float32) * DIM ** (-0.5)
        bout = jnp.zeros((DIM,), dtype=jnp.float32)
        graph_bias = jax.random.normal(ks[5], (1, 1, 1), dtype=jnp.float32) * 0.1
        return {'x': x, 'adj_matrix': adj_matrix, 'attn_mask': attn_mask, 'Wqkv': Wqkv, 'bqkv': bqkv, 'Wout': Wout, 'bout': bout, 'graph_bias': graph_bias}
    _L1_gnn_all = _L1_gnn_setup()
    _L1_gnn_in = {k: v for k, v in _L1_gnn_all.items() if k in ('Wqkv', 'bqkv', 'Wout', 'bout', 'graph_bias')}
    del _L1_gnn_all

    def _L1_ffn_setup():
        import jax, jax.numpy as jnp
        import numpy as np
        D_MODEL = 128
        EXPERT_DIM = 256
        NUM_EXPERTS = 8
        TOP_K = 2
        SEQ_LEN = 1024
        BATCH = 2
        key = jax.random.key(seed)
        ks = jax.random.split(key, 8)
        s = 0.02
        x = jax.random.normal(ks[0], (SEQ_LEN, BATCH, D_MODEL), dtype=jnp.float32)
        Wg = jax.random.normal(ks[1], (D_MODEL, NUM_EXPERTS), dtype=jnp.float32) * s
        bg = jax.random.normal(ks[2], (NUM_EXPERTS,), dtype=jnp.float32) * s
        bias = jnp.zeros((NUM_EXPERTS,), dtype=jnp.float32)
        W1 = jax.random.normal(ks[3], (NUM_EXPERTS, D_MODEL, EXPERT_DIM), dtype=jnp.float32) * s
        b1 = jax.random.normal(ks[4], (NUM_EXPERTS, EXPERT_DIM), dtype=jnp.float32) * s
        W2 = jax.random.normal(ks[5], (NUM_EXPERTS, EXPERT_DIM, D_MODEL), dtype=jnp.float32) * s
        b2 = jax.random.normal(ks[6], (NUM_EXPERTS, D_MODEL), dtype=jnp.float32) * s
        return {'x': x, 'Wg': Wg, 'bg': bg, 'bias': bias, 'W1': W1, 'b1': b1, 'W2': W2, 'b2': b2}
    _L1_ffn_all = _L1_ffn_setup()
    _L1_ffn_in = {k: v for k, v in _L1_ffn_all.items() if k in ('Wg', 'bg', 'bias', 'W1', 'b1', 'W2', 'b2')}
    del _L1_ffn_all
    return {'x': x, 'adj': adj, 'L0_gnn_spatial_x': _L0_gnn_in['spatial_x'], 'L0_gnn_W_f': _L0_gnn_in['W_f'], 'L0_gnn_b_f': _L0_gnn_in['b_f'], 'L0_gnn_W_s': _L0_gnn_in['W_s'], 'L0_gnn_b_s': _L0_gnn_in['b_s'], 'L0_gnn_W_att': _L0_gnn_in['W_att'], 'L0_gnn_b_att': _L0_gnn_in['b_att'], 'L0_ffn_U_i': _L0_ffn_in['U_i'], 'L0_ffn_V_i': _L0_ffn_in['V_i'], 'L0_ffn_b_i': _L0_ffn_in['b_i'], 'L0_ffn_U_f': _L0_ffn_in['U_f'], 'L0_ffn_V_f': _L0_ffn_in['V_f'], 'L0_ffn_b_f': _L0_ffn_in['b_f'], 'L0_ffn_U_c': _L0_ffn_in['U_c'], 'L0_ffn_V_c': _L0_ffn_in['V_c'], 'L0_ffn_b_c': _L0_ffn_in['b_c'], 'L0_ffn_U_o': _L0_ffn_in['U_o'], 'L0_ffn_V_o': _L0_ffn_in['V_o'], 'L0_ffn_b_o': _L0_ffn_in['b_o'], 'L1_gnn_Wqkv': _L1_gnn_in['Wqkv'], 'L1_gnn_bqkv': _L1_gnn_in['bqkv'], 'L1_gnn_Wout': _L1_gnn_in['Wout'], 'L1_gnn_bout': _L1_gnn_in['bout'], 'L1_gnn_graph_bias': _L1_gnn_in['graph_bias'], 'L1_ffn_Wg': _L1_ffn_in['Wg'], 'L1_ffn_bg': _L1_ffn_in['bg'], 'L1_ffn_bias': _L1_ffn_in['bias'], 'L1_ffn_W1': _L1_ffn_in['W1'], 'L1_ffn_b1': _L1_ffn_in['b1'], 'L1_ffn_W2': _L1_ffn_in['W2'], 'L1_ffn_b2': _L1_ffn_in['b2']}

def reference(x, adj, L0_gnn_spatial_x, L0_gnn_W_f, L0_gnn_b_f, L0_gnn_W_s, L0_gnn_b_s, L0_gnn_W_att, L0_gnn_b_att, L0_ffn_U_i, L0_ffn_V_i, L0_ffn_b_i, L0_ffn_U_f, L0_ffn_V_f, L0_ffn_b_f, L0_ffn_U_c, L0_ffn_V_c, L0_ffn_b_c, L0_ffn_U_o, L0_ffn_V_o, L0_ffn_b_o, L1_gnn_Wqkv, L1_gnn_bqkv, L1_gnn_Wout, L1_gnn_bout, L1_gnn_graph_bias, L1_ffn_Wg, L1_ffn_bg, L1_ffn_bias, L1_ffn_W1, L1_ffn_b1, L1_ffn_W2, L1_ffn_b2):
    import jax
    import jax.numpy as jnp

    def _L0_gnn_ref(feature_x, spatial_x, adj, W_f, b_f, W_s, b_s, W_att, b_att):
        import jax, jax.numpy as jnp
        import numpy as np
        N, IN_DIM, HID = (4096, 128, 128)

        def _gcn_layer(x, adj, W, b):
            d_inv_sqrt = (jnp.sum(adj, axis=1) + 1e-09) ** (-0.5)
            msg = d_inv_sqrt[:, None] * adj * d_inv_sqrt[None, :] @ x
            return jax.nn.relu(msg @ W + b)
        H_f = _gcn_layer(feature_x, adj, W_f, b_f)
        H_s = _gcn_layer(spatial_x, adj, W_s, b_s)
        H_cat = jnp.concatenate([H_f, H_s], axis=1)
        attn = jax.nn.sigmoid(H_cat @ W_att + b_att)
        return attn * H_f + (1.0 - attn) * H_s

    def _L0_ffn_ref(x, U_i, V_i, b_i, U_f, V_f, b_f, U_c, V_c, b_c, U_o, V_o, b_o):
        import jax, jax.numpy as jnp
        import numpy as np
        from jax import lax
        B, T, _ = x.shape
        H = U_i.shape[1]
        xt = jnp.swapaxes(x, 0, 1)
        xi = xt @ U_i + b_i
        xf = xt @ U_f + b_f
        xg = xt @ U_c + b_c
        xo = xt @ U_o + b_o
        h0 = jnp.zeros((B, H), x.dtype)
        c0 = jnp.zeros((B, H), x.dtype)

        def step(carry, xs):
            h, c = carry
            xi_t, xf_t, xg_t, xo_t = xs
            i_t = jax.nn.sigmoid(xi_t + h @ V_i)
            f_t = jax.nn.sigmoid(xf_t + h @ V_f)
            g_t = jnp.tanh(xg_t + h @ V_c)
            o_t = jax.nn.sigmoid(xo_t + h @ V_o)
            c_new = h * c + i_t * g_t
            h_new = o_t * jnp.tanh(c_new)
            return ((h_new, c_new), h_new)
        (_, _), hs = lax.scan(step, (h0, c0), (xi, xf, xg, xo))
        return jnp.swapaxes(hs, 0, 1)

    def _L1_gnn_ref(x, adj_matrix, attn_mask, Wqkv, bqkv, Wout, bout, graph_bias):
        import jax, jax.numpy as jnp
        import numpy as np
        N = 4096
        DIM = 128
        HEADS = 4
        HD = DIM // HEADS
        SCALE = HD ** (-0.5)
        n, d = x.shape
        qkv = x @ Wqkv + bqkv
        q, k, v = jnp.split(qkv, 3, axis=-1)

        def split_heads(t):
            return t.reshape(n, HEADS, HD).transpose(1, 0, 2)
        qh, kh, vh = (split_heads(q), split_heads(k), split_heads(v))
        scores = jnp.einsum('hnd,hmd->hnm', qh, kh) * SCALE
        scores = scores + graph_bias * adj_matrix[None, :, :]
        scores = jnp.where(attn_mask[None, :, :] == 0, jnp.float32(-1000000000.0), scores)
        attn = jax.nn.softmax(scores, axis=-1)
        out = jnp.einsum('hnm,hmd->hnd', attn, vh)
        out = out.transpose(1, 0, 2).reshape(n, d)
        return out @ Wout + bout

    def _L1_ffn_ref(x, Wg, bg, bias, W1, b1, W2, b2):
        import jax, jax.numpy as jnp
        import numpy as np
        D_MODEL = 128
        EXPERT_DIM = 256
        NUM_EXPERTS = 8
        TOP_K = 2
        SEQ_LEN = 1024
        BATCH = 2
        x_flat = x.reshape(-1, D_MODEL)
        gate_logits = x_flat @ Wg + bg + bias
        topk_vals, topk_idx = jax.lax.top_k(gate_logits, TOP_K)
        topk_w = jax.nn.softmax(topk_vals, axis=-1)
        combine = (jax.nn.one_hot(topk_idx, NUM_EXPERTS, dtype=x.dtype) * topk_w[..., None]).sum(axis=1)
        h = jax.nn.relu(jnp.einsum('td,edh->teh', x_flat, W1) + b1)
        y = jnp.einsum('teh,ehd->ted', h, W2) + b2
        out = jnp.einsum('ted,te->td', y, combine)
        return out.reshape(x.shape)
    x = x + _L0_gnn_ref(_layernorm(x, axis=-1), L0_gnn_spatial_x, adj, L0_gnn_W_f, L0_gnn_b_f, L0_gnn_W_s, L0_gnn_b_s, L0_gnn_W_att, L0_gnn_b_att)
    x = x + _L0_ffn_ref(_layernorm(x, axis=-1)[None], L0_ffn_U_i, L0_ffn_V_i, L0_ffn_b_i, L0_ffn_U_f, L0_ffn_V_f, L0_ffn_b_f, L0_ffn_U_c, L0_ffn_V_c, L0_ffn_b_c, L0_ffn_U_o, L0_ffn_V_o, L0_ffn_b_o)[0]
    x = x + _L1_gnn_ref(_layernorm(x, axis=-1), adj, adj, L1_gnn_Wqkv, L1_gnn_bqkv, L1_gnn_Wout, L1_gnn_bout, L1_gnn_graph_bias)
    x = x + _L1_ffn_ref(_layernorm(x, axis=-1)[None], L1_ffn_Wg, L1_ffn_bg, L1_ffn_bias, L1_ffn_W1, L1_ffn_b1, L1_ffn_W2, L1_ffn_b2)[0]
    return x

_drawn_inputs = setup_inputs


def setup_inputs(seed=0):
    import zlib

    import numpy as np

    out = dict(_drawn_inputs(seed))
    spreads = {'L1_gnn_bqkv': (0.0, 0.1), 'L1_gnn_bout': (0.0, 0.1), 'L1_ffn_bias': (0.0, 0.418)}
    factors = {'L0_gnn_W_att': 37.479,
     'L0_ffn_V_i': 8.0,
     'L0_ffn_b_i': 8.0,
     'L0_ffn_V_c': 3.522,
     'L0_ffn_b_c': 3.321,
     'L0_ffn_V_o': 8.0,
     'L0_ffn_b_o': 8.0,
     'L1_ffn_bg': 6.348,
     'L1_ffn_b1': 8.0,
     'L1_ffn_b2': 4.159}
    for name, (base, spread) in spreads.items():
        noise = np.random.default_rng([zlib.crc32(name.encode()), seed]).standard_normal(out[name].shape)
        drawn = base * np.exp(spread * noise) if base else spread * noise
        out[name] = jnp.asarray(drawn.astype(out[name].dtype))
    for name, factor in factors.items():
        out[name] = (out[name] * factor).astype(out[name].dtype)
    return out
```

```python
from contextlib import ExitStack

import numpy as np

import concourse.bass as bass
from concourse import mybir
from concourse.bass import ds

F32 = mybir.dt.float32
F16 = mybir.dt.float16
U32 = mybir.dt.uint32
ALU = mybir.AluOpType
ACT = mybir.ActivationFunctionType
AX_X = mybir.AxisListType.X

P = 128
N = 4096
TILES = N // P
GROUP = 4
GROUPS = TILES // GROUP
GW = GROUP * P
EPS = 1e-5
DEG_EPS = 1e-9
MASKED = -1e9
HEADS = 4
HD = P // HEADS
SCALE = HD ** -0.5
EXPERTS = 8
HID = 256
HT = EXPERTS * HID // P
STEPS = 16
BODY = 4 * STEPS
HALF = N // 2
UT = HALF // P
PAIR = 1024


def wait_apart(eng, signal, value):
    reg = eng.to_reg(value)
    eng.wait_ge(signal, 0)
    eng.wait_ge(signal, reg)

G_LINKS, P_LINKS, M_LINKS, E_LINKS = 24, 11, 28, 24


class Chain:

    def __init__(self, eng, sem, base=0):
        self.eng, self.sem, self.base, self.n = eng, sem, base, 0

    def __call__(self, ins, apart=False):
        self.n += 1
        ins.then_inc(self.sem, 1)
        if apart:
            wait_apart(self.eng, self.sem, self.base + self.n)
        else:
            self.eng.wait_ge(self.sem, self.base + self.n)


def build(nc, d, out):
    ctx = ExitStack()
    with ctx:
        def sb(name, shape, dt=F32):
            return ctx.enter_context(nc.sbuf_tensor(name, shape, dt))

        def sem(name):
            return ctx.enter_context(nc.semaphore(name))

        x = sb("x", [P, TILES, P])
        ident = sb("ident", [P, P])
        rows = sb("rows", [P, 6, P])
        gcn_w = sb("gcn_w", [P, 2, P])
        cols = sb("cols", [P, 10])
        gate_rows = sb("gate_rows", [P, 3, 8])
        scan_b = sb("scan_b", [1, 3, P])
        w_out = sb("w_out", [P, HEADS * P])
        e_b1 = sb("e_b1", [P, HT])
        e_b2 = sb("e_b2", [EXPERTS, P])
        e_wg = sb("e_wg", [P, EXPERTS])
        arena = sb("arena", [P, 43008])
        psum = ctx.enter_context(nc.psum_tensor("psum", [P, 8, 512], F32))
        b_f, b_s, wa_f, wa_s, b_out, b_v = (rows[:, k, :] for k in range(6))
        b_att, g_bias = cols[:, 0:1], cols[:, 1:2]

        def view(at, shape, dt=F32):
            n = int(np.prod(shape)) // (2 if dt == F16 else 1)
            ap = arena[:, at:at + n]
            if dt == F16:
                ap = ap.bitcast(F16)
            if len(shape) == 2:
                ap = ap.rearrange("p (a b) -> p a b", a=shape[0])
            if len(shape) == 3:
                ap = ap.rearrange("p (a b c) -> p a b c", a=shape[0], b=shape[1])
            return ap

        stage = view(0, [4, N])
        feat = view(16384, [TILES, 2 * P])
        hs_t = view(20480, [N])
        xn_t = view(24576, [N + BODY])
        msg_t = view(28736, [2, GW])
        cen = view(29760, [GROUP, P])
        hs_g = view(30272, [GROUP, P])
        wrk = view(30784, [GROUP, P])
        nrm = view(31296, [GROUP, P])
        scan_v = view(31808, [3, P])
        scan_u = view(32192, [3, P])
        v_res = view(32576, [3, P])
        v_hi = view(32960, [3, P], F16)
        v_lo = view(33152, [3, P], F16)
        v_nat = view(0, [TILES, P])
        q_st = view(4096, [HEADS, N], F16)
        k_st = view(12288, [HEADS, N], F16)
        prep_t = view(28736, [GW])
        h_stage = view(29248, [GW])
        prep_qk = view(32576, [2, GW])
        prep_w = view(36864, [2 * HEADS + 1, P])
        score = view(20480, [2, HEADS, HALF])
        bias_a = view(36864, [2, HALF])
        p_t = view(40960, [4, GW])
        mask = sb("mask", [P, 512])
        o_t = sb("o_t", [P, P])
        y0 = sb("y0", [P, HEADS * P])
        e_w1 = view(0, [EXPERTS * HID])
        e_w2 = view(2048, [HT, P])
        xe_t = view(4096, [GW])
        e_cen = view(4608, [GROUP, P])
        e_wrk = view(5120, [GROUP, P])
        hid_t = view(8192, [HT, GW])
        deg = sb("deg", [P, TILES])
        dinv = sb("dinv", [P, TILES])
        st = sb("st", [P, 4, TILES])
        small = sb("small", [P, 8, GROUP])
        ones = sb("ones", [1, STEPS])
        neg_one = sb("neg_one", [P, 1])
        h_hi = sb("h_hi", [P, 1], F16)
        h_lo = sb("h_lo", [P, 1], F16)
        hc = sb("hc", [P, 1])
        cell = sb("cell", [P, 1])
        h_new = sb("h_new", [P, BODY])
        tables = sb("tables", [P, 1])
        gates_of = sb("gates", [P, 2, 2])
        mx = sb("mx", [P, HEADS, 2])
        nmx = sb("nmx", [P, 2, HEADS])
        lsum = sb("lsum", [P, 2, HEADS])
        fac = sb("fac", [P, 6, 2 * HEADS])
        lg = sb("lg", [P, GROUP, 8])
        top = sb("top", [P, GROUP, 8])
        top_i = sb("top_i", [P, GROUP, 8], U32)
        top_f = sb("top_f", [P, GROUP, 8])
        pw = sb("pw", [P, 4, GROUP])
        comb = sb("comb", [P, GROUP, EXPERTS])
        comb2 = sb("comb2", [P, GROUP, EXPERTS])
        comb_t = sb("comb_t", [EXPERTS, GW])

        names = """consts_in x_in adj_in_0 adj_in_1 adj_in_2 adj_in_3 adj_summed
        adj_t_in_0 adj_t_in_1 adj_t_in_2 adj_t_in_3 msg_done msg_a msg_v h_done
        gate_in gate_out rs_in rs_out ln_done xt_done xt_out g_chain s_chain s2_chain
        setup scan_z scan_zg scan_kept scan_io scan_t scan_hi scan_lo scan_h scan_hc
        ht_in ht_done p_rs_in p_rs_out p_ln p_xt p_xt_out p_qk p_qk32 p_hi p_split p_v p_v_out p_chain scaled
        prepw_in bias_in_0 bias_in_1 masked bias_ready qk_done ttr_done nm_done exp_done tp_done ev_act ev_dve pv_done
        o_out y_done y0_out y_used fac_in fac_out f_chain c_chain tile_done
        m_rs_in m_rs_out m_ln m_xt m_xt_out m_lg m_ex_in m_ex_out m_comb m_ct m_ct_out m_chain
        expw_in e_h e_hid e_y e_used e_chain stored""".split()
        s = {k: sem(k) for k in names}

        block = ctx.enter_context(nc.Block())

        x_rows = d["x"].rearrange("(t p) f -> p t f", p=P)
        sp_rows = d["spatial"].rearrange("(t p) f -> p t f", p=P)
        adj_rows = d["adj"].rearrange("(t p) m -> p t m", p=P)
        adj_t = d["adj_t"].rearrange("(b p) n -> p b n", p=P)
        out_rows = out.rearrange("(t p) f -> p t f", p=P)
        consts = ((ident[:], "ident"), (rows[:], "rows"), (gcn_w[:], "gcn_w"), (cols[:], "cols"),
                  (gate_rows[:], "gate_rows"), (scan_b[:], "scan_b"), (scan_v, "scan_v"), (scan_u, "scan_u"),
                  (w_out[:], "w_out"), (e_b1[:], "e_b1"), (e_b2[:], "e_b2"), (e_wg[:], "e_wg"))

        def over_rows(row):
            return row.unsqueeze(1).to_broadcast([P, GROUP, P])

        def over_cols(col, n=GROUP, w=P):
            return col.unsqueeze(2).to_broadcast([P, n, w])

        def tiles_of(bank):
            return psum[:, bank, :].rearrange("p (t f) -> p t f", f=P)

        V_TILES = ((1,), (5,), (9,), (13, 15))
        V_ALL = [g for q in V_TILES for g in q]

        def wait_past(eng, signal, base, more):
            if not isinstance(base, int) or base + more > 0:
                eng.wait_ge(signal, base + more)

        def wait_evacuated(eng, n_unit, g):
            if g in V_ALL:
                eng.wait_ge(s["ev_dve"], n_unit * len(V_ALL) + V_ALL.index(g) + 1)
            else:
                mine = [k for k in range(UT) if k not in V_ALL]
                eng.wait_ge(s["ev_act"], n_unit * len(mine) + mine.index(g) + 1)

        @block.sync
        def _(e):
            e.dma_start(x[:], x_rows).then_inc(s["x_in"], 16)
            e.dma_start(feat[:, :, P:2 * P], sp_rows).then_inc(s["x_in"], 16)
            for dst, src in consts:
                e.dma_start(dst, d[src]).then_inc(s["consts_in"], 16)
            for k in range(4):
                e.dma_start(stage[:, k, :], adj_rows[:, k, :]).then_inc(s["adj_in_%d" % k], 16)
            with e.Fori(1, TILES // 4) as i:
                for k in range(4):
                    e.wait_ge(s["adj_summed"], i * 4 + (k - 3))
                    e.dma_start(stage[:, k, :].unsqueeze(1), adj_rows[:, ds(i * 4 + k, 1), :]
                                ).then_inc(s["adj_in_%d" % k], 16)
            for k in range(4):
                e.wait_ge(s["adj_summed"], TILES - 3 + k)
                e.dma_start(stage[:, k, :].rearrange("p (b n) -> p b n", b=8),
                            adj_t[:, 8 * k:8 * k + 8, 0:GW]).then_inc(s["adj_t_in_%d" % k], 16)
            with e.Fori(1, GROUPS) as j:
                for k in range(4):
                    e.wait_ge(s["msg_done"], j * 4 + (k - 3))
                    e.dma_start(stage[:, k, :].rearrange("p (b n) -> p b n", b=8),
                                adj_t[:, 8 * k:8 * k + 8, ds(j * GW, GW)]).then_inc(s["adj_t_in_%d" % k], 16)
            e.wait_ge(s["setup"], 2)
            e.dma_start(prep_w, d["qkv_w"]).then_inc(s["prepw_in"], 16)
            e.wait_ge(s["p_qk"], GROUPS * 2 * HEADS)
            e.wait_ge(s["p_v"], GROUPS)
            for k in range(2):
                e.dma_start(bias_a[:, k, :], adj_rows[:, 0, k * HALF:(k + 1) * HALF]).then_inc(s["bias_in_%d" % k], 16)
            with e.Fori(1, TILES) as t:
                for k in range(2):
                    e.wait_ge(s["ttr_done"], t * 16 + (k - 1) * 8)
                    e.dma_start(bias_a[:, k, :].unsqueeze(1),
                                adj_rows[:, ds(t, 1), k * HALF:(k + 1) * HALF]).then_inc(s["bias_in_%d" % k], 16)
            e.wait_ge(s["pv_done"], 2 * TILES * UT)
            e.dma_start(e_w1, d["e_w1"]).then_inc(s["expw_in"], 16)
            e.dma_start(e_w2, d["e_w2"]).then_inc(s["expw_in"], 16)
            with e.Fori(0, GROUPS) as j:
                e.wait_ge(s["e_used"], (j + 1) * 3 * GROUP)
                e.dma_start(out_rows[:, ds(j * GROUP, GROUP), :], x[:, ds(j * GROUP, GROUP), :]
                            ).then_inc(s["stored"], 16)
            e.wait_ge(s["stored"], 16 * GROUPS)

        def centre(v, link, src, dst, tmp, mean, var, ready):
            link(v.tensor_reduce(mean, src, AX_X, ALU.add))
            link(v.tensor_scalar(mean, mean, 1.0 / P, None, ALU.mult))
            link(v.tensor_tensor(dst, src, over_cols(mean, dst.shape[1]), ALU.subtract))
            link(v.tensor_tensor(tmp, dst, dst, ALU.mult))
            link(v.tensor_reduce(var, tmp, AX_X, ALU.add))
            v.tensor_scalar(var, var, 1.0 / P, EPS, ALU.mult, ALU.add).then_inc(ready, 1)

        def rsqrt(v, link, a, root, r, t):
            link(v.reciprocal(r, root))
            link(v.tensor_tensor(t, r, r, ALU.mult))
            link(v.tensor_tensor(t, t, a, ALU.mult))
            link(v.tensor_scalar(t, t, -0.5, 1.5, ALU.mult, ALU.add))
            link(v.tensor_tensor(r, r, t, ALU.mult))

        @block.vector
        def _(v):
            link = Chain(v, s["s_chain"])
            v.wait_ge(s["x_in"], 32)
            v.wait_ge(s["consts_in"], 16 * len(consts))
            centre(v, link, x[:], feat[:, :, 0:P], xn_t[:, 0:N].rearrange("p (t f) -> p t f", f=P),
                   st[:, 0, :], st[:, 1, :], s["rs_in"])
            v.wait_ge(s["rs_out"], 1)
            rsqrt(v, link, st[:, 1, :], st[:, 2, :], st[:, 3, :], st[:, 0, :])
            link(v.tensor_tensor(feat[:, :, 0:P], feat[:, :, 0:P], over_cols(st[:, 3, :], TILES), ALU.mult))
            with v.Fori(0, TILES // 4) as i:
                for k in range(4):
                    wait_apart(v, s["adj_in_%d" % k], (i + 1) * 16)
                    v.tensor_reduce(deg[:, ds(i * 4 + k, 1)], stage[:, k, :], AX_X, ALU.add
                                    ).then_inc(s["adj_summed"], 1)
            link = Chain(v, s["s2_chain"])
            v.wait_ge(s["adj_summed"], TILES)
            v.tensor_scalar(deg[:], deg[:], DEG_EPS, None, ALU.add).then_inc(s["rs_in"], 1)
            v.wait_ge(s["rs_out"], 2)
            rsqrt(v, link, deg[:], st[:, 2, :], dinv[:], st[:, 0, :])
            v.tensor_tensor(feat, feat, over_cols(dinv[:], TILES, 2 * P), ALU.mult).then_inc(s["setup"], 1)
            link(v.tensor_copy(v_hi, scan_v))
            link(v.tensor_tensor(v_res, scan_v, v_hi, ALU.subtract))
            link(v.tensor_copy(v_lo, v_res))
            link(v.memset(ones[:], 1.0))
            link(v.memset(xn_t[:, N:], 0.0))
            v.memset(hc[:], 0.0).then_inc(s["scan_hc"], 1)
            v.memset(h_hi[:], 0.0).then_inc(s["scan_hi"], 1)
            v.memset(h_lo[:], 0.0).then_inc(s["scan_lo"], 1)
            v.memset(neg_one[:], -1.0).then_inc(s["setup"], 1)

            hf = cen
            with v.Fori(0, GROUPS) as j:
                link = Chain(v, s["g_chain"], j * G_LINKS)
                xg = x[:, ds(j * GROUP, GROUP), :]
                dg = over_cols(dinv[:, ds(j * GROUP, GROUP)])
                v.wait_ge(s["msg_done"], j * 4 + 4)
                v.tensor_copy(msg_t[:, 1, :], psum[:, 1, :]).then_inc(s["msg_v"], 1)
                v.wait_ge(s["h_done"], j + 1)
                for h, bank, bias in ((hf, 2, b_f), (hs_g, 3, b_s)):
                    link(v.tensor_tensor(h, tiles_of(bank), dg, ALU.mult))
                    link(v.tensor_tensor(h, h, over_rows(bias), ALU.add))
                    link(v.tensor_scalar(h, h, 0.0, None, ALU.max))
                for k, h, w in ((0, hf, wa_f), (1, hs_g, wa_s)):
                    link(v.tensor_tensor(wrk, h, over_rows(w), ALU.mult))
                    link(v.tensor_reduce(small[:, k, :], wrk, AX_X, ALU.add))
                v.tensor_tensor(small[:, 2, :], small[:, 0, :], small[:, 1, :], ALU.add).then_inc(s["gate_in"], 1)
                link(v.tensor_tensor(hf, hf, hs_g, ALU.subtract))
                link(v.tensor_tensor(xg, xg, hs_g, ALU.add))
                v.wait_ge(s["gate_out"], j + 1)
                link(v.tensor_tensor(hf, hf, over_cols(small[:, 3, :]), ALU.mult))
                link(v.tensor_tensor(xg, xg, hf, ALU.add), True)
                centre(v, link, xg, cen, wrk, small[:, 4, :], small[:, 5, :], s["rs_in"])
                v.wait_ge(s["rs_out"], j + 3)
                rsqrt(v, link, small[:, 5, :], small[:, 6, :], small[:, 7, :], small[:, 4, :])
                v.tensor_tensor(nrm, cen, over_cols(small[:, 7, :]), ALU.mult).then_inc(s["ln_done"], 1)
                assert link.n == G_LINKS

            v.wait_ge(s["ln_done"], GROUPS)
            with v.Fori(0, N // BODY) as i:
                for k in range(BODY):
                    t1 = i * BODY + (k + 1)
                    tanh_c, gates, h_k = psum[:, 5, 0:1], gates_of[:, k % 2, :], h_new[:, k:k + 1]
                    v.wait_ge(s["scan_t"], t1)
                    v.tensor_tensor(h_hi[:], gates[:, 1:2], tanh_c, ALU.mult).then_inc(s["scan_hi"], 1)
                    v.wait_ge(s["scan_hi"], t1 + 1)
                    v.scalar_tensor_tensor(h_lo[:], tanh_c, gates[:, 1:2], h_hi[:], ALU.mult, ALU.subtract
                                           ).then_inc(s["scan_lo"], 1)
                    v.scalar_tensor_tensor(cell[:], psum[:, 4 + 2 * (k % 2), 0:1], gates[:, 0:1], hc[:],
                                           ALU.mult, ALU.add)
                    v.tensor_tensor(h_k, gates[:, 1:2], tanh_c, ALU.mult).then_inc(s["scan_h"], 1)
                    v.wait_ge(s["scan_h"], t1)
                    v.tensor_tensor(hc[:], h_k, cell[:], ALU.mult).then_inc(s["scan_hc"], 1)
                v.tensor_copy(hs_t[:, ds(i * BODY, BODY)], h_new[:]).then_inc(s["scan_kept"], 1)

            v.wait_ge(s["scan_kept"], N // BODY)
            v.tensor_scalar(cols[:, 2:6], cols[:, 2:6], SCALE, None, ALU.mult).then_inc(s["scaled"], 1)
            with v.Fori(0, GROUPS) as j:
                link = Chain(v, s["p_chain"], j * P_LINKS)
                xg = x[:, ds(j * GROUP, GROUP), :]
                v.tensor_copy(h_stage, hs_t[:, ds(j * GW, GW)]).then_inc(s["ht_in"], 1)
                v.wait_ge(s["ht_done"], j + 1)
                link(v.tensor_tensor(xg, xg, tiles_of(0), ALU.add), True)
                centre(v, link, xg, cen, wrk, small[:, 4, :], small[:, 5, :], s["p_rs_in"])
                v.wait_ge(s["p_rs_out"], j + 1)
                rsqrt(v, link, small[:, 5, :], small[:, 6, :], small[:, 7, :], small[:, 4, :])
                v.tensor_tensor(nrm, cen, over_cols(small[:, 7, :]), ALU.mult).then_inc(s["p_ln"], 1)
                v.wait_ge(s["p_v"], j + 1)
                v.tensor_tensor(v_nat[:, ds(j * GROUP, GROUP), :], tiles_of(2), over_rows(b_v), ALU.add
                                ).then_inc(s["p_v_out"], 1)
                for h in range(2 * HEADS):
                    dst = (q_st if h < HEADS else k_st)[:, h % HEADS, ds(j * GW, GW)]
                    src = prep_qk[:, h % 2, :]
                    v.wait_ge(s["p_qk32"], j * 8 + h + 1)
                    v.tensor_copy(dst, src).then_inc(s["p_hi"], 1)
                    v.wait_ge(s["p_hi"], j * 8 + h + 1)
                    if h < HEADS:
                        v.tensor_tensor(dst[64:128], src[64:128], dst[64:128], ALU.subtract
                                        ).then_inc(s["p_split"], 2)
                    else:
                        for q in (32, 96):
                            v.tensor_tensor(dst[q:q + 32], src[q:q + 32], dst[q:q + 32], ALU.subtract
                                            ).then_inc(s["p_split"], 1)
                assert link.n == P_LINKS

            def bias_quarter(t, half, q):
                u = 2 * t + half
                if q == 0:
                    v.wait_ge(s["bias_in_%d" % half], (t + 1) * 16)
                c = bias_a[:, half, q * 512:(q + 1) * 512]
                v.wait_ge(s["bias_ready"], u * 4 + q)
                v.tensor_scalar(mask[:], c, 0.0, MASKED, ALU.is_equal, ALU.mult).then_inc(s["masked"], 1)
                v.wait_ge(s["masked"], u * 4 + q + 1)
                v.scalar_tensor_tensor(c, c, g_bias, mask[:], ALU.mult, ALU.add).then_inc(s["bias_ready"], 1)

            def evacuate_v(u, g):
                v.wait_ge(s["tp_done"], u * UT + g + 1)
                wait_past(v, s["pv_done"], u * UT, g - 3)
                v.tensor_copy(p_t[:, g % 4, :], psum[:, 4 + g % 2, :]).then_inc(s["ev_dve"], 1)

            def factors_in(t):
                link = Chain(v, s["f_chain"], t * 6)
                m0, m1 = nmx[:, 0, :], nmx[:, 1, :]
                link(v.tensor_tensor(fac[:, 0, 0:4], m0, m1, ALU.min))
                link(v.tensor_tensor(fac[:, 1, 0:4], fac[:, 0, 0:4], m0, ALU.subtract))
                v.tensor_tensor(fac[:, 1, 4:8], fac[:, 0, 0:4], m1, ALU.subtract).then_inc(s["fac_in"], 1)
                return link

            def factors_out(t, link):
                v.wait_ge(s["fac_out"], t + 1)
                link(v.tensor_tensor(fac[:, 3, :], fac[:, 2, :], lsum[:].rearrange("p a h -> p (a h)"), ALU.mult))
                link(v.tensor_tensor(fac[:, 4, 0:4], fac[:, 3, 0:4], fac[:, 3, 4:8], ALU.add))
                link(v.reciprocal(fac[:, 4, 4:8], fac[:, 4, 0:4]))
                link(v.tensor_tensor(fac[:, 5, :].rearrange("p (a h) -> p a h", a=2),
                                     fac[:, 2, :].rearrange("p (a h) -> p a h", a=2),
                                     fac[:, 4, 4:8].unsqueeze(1).to_broadcast([P, 2, HEADS]), ALU.mult))
                assert link.n == 6, link.n

            def combine(t):
                link = Chain(v, s["c_chain"], t * 8)
                xt = x[:, ds(t, 1), :].rearrange("p a f -> p (a f)")
                link(v.tensor_tensor(xt, xt, b_out, ALU.add))
                v.wait_ge(s["y0_out"], t + 1)
                for h in range(HEADS):
                    link(v.scalar_tensor_tensor(xt, y0[:, h * P:(h + 1) * P], fac[:, 5, h:h + 1], xt,
                                                ALU.mult, ALU.add))
                v.wait_ge(s["y_done"], 2 * t + 2)
                for h in range(HEADS - 1):
                    link(v.scalar_tensor_tensor(xt, psum[:, 7, h * P:(h + 1) * P], fac[:, 5, 4 + h:5 + h], xt,
                                                ALU.mult, ALU.add))
                v.scalar_tensor_tensor(xt, psum[:, 7, 3 * P:4 * P], fac[:, 5, 7:8], xt, ALU.mult, ALU.add
                                       ).then_inc(s["tile_done"], 1)
                assert link.n == 8, link.n

            def unit_v(t, half, before, after):
                u = t * 2 + half
                v.wait_ge(s["bias_ready"], (u + 1) * 4)
                for h in range(HEADS):
                    for q in range(2):
                        n = u * 8 + 2 * h + q
                        c = slice(q * PAIR, (q + 1) * PAIR)
                        wait_apart(v, s["qk_done"], n + 1)
                        v.tensor_tensor_reduce(score[:, half, h, c].rearrange("p (a b) -> p a b", a=2),
                                               psum[:, 2 * q:2 * q + 2, :],
                                               bias_a[:, half, c].rearrange("p (a b) -> p a b", a=2),
                                               1.0, -3e38, ALU.add, ALU.max, mx[:, h, q:q + 1]
                                               ).then_inc(s["ttr_done"], 1)
                    if h == 0 and half == 0 and before:
                        v.wait_ge(s["exp_done"], u * HEADS)
                        factors_out(t - 1, factors_in(t - 1))
                    if h == 0 and half == 1 and before:
                        combine(t - 1)
                    v.wait_ge(s["ttr_done"], u * 8 + 2 * h + 2)
                    v.scalar_tensor_tensor(nmx[:, half, h:h + 1], mx[:, h, 0:1], mx[:, h, 1:2], neg_one[:],
                                           ALU.max, ALU.mult).then_inc(s["nm_done"], 1)
                    if before or half:
                        for g in V_TILES[h]:
                            evacuate_v(u - 1, g)
                    if after or not half:
                        for q in ((), (0,), (1,), (2, 3))[h]:
                            bias_quarter(t + half, 1 - half, q)

            v.wait_ge(s["p_split"], GROUPS * 2 * 2 * HEADS)
            for q in range(4):
                bias_quarter(0, 0, q)
            for half in range(2):
                unit_v(0, half, False, True)
            with v.Fori(1, TILES - 1) as t:
                for half in range(2):
                    unit_v(t, half, True, True)
            for half in range(2):
                unit_v(TILES - 1, half, True, False)
            v.wait_ge(s["exp_done"], 2 * TILES * HEADS)
            factors_out(TILES - 1, factors_in(TILES - 1))
            for g in V_ALL:
                evacuate_v(2 * TILES - 1, g)
            combine(TILES - 1)

            v.wait_ge(s["tile_done"], TILES)
            with v.Fori(0, GROUPS) as j:
                link = Chain(v, s["m_chain"], j * M_LINKS)
                xg = x[:, ds(j * GROUP, GROUP), :]
                centre(v, link, xg, e_cen, e_wrk, small[:, 4, :], small[:, 5, :], s["m_rs_in"])
                v.wait_ge(s["m_rs_out"], j + 1)
                rsqrt(v, link, small[:, 5, :], small[:, 6, :], small[:, 7, :], small[:, 4, :])
                v.tensor_tensor(e_wrk, e_cen, over_cols(small[:, 7, :]), ALU.mult).then_inc(s["m_ln"], 1)
                v.wait_ge(s["m_lg"], j + 1)
                for k in range(2):
                    acc = psum[:, 1, 0:GROUP * 8].rearrange("p (t f) -> p t f", f=8)
                    link(v.tensor_tensor(lg[:], lg[:] if k else acc,
                                         gate_rows[:, k, :].unsqueeze(1).to_broadcast([P, GROUP, 8]), ALU.add),
                         k == 1)
                for k in range(GROUP):
                    link(v.max(top[:, k, :], lg[:, k, :]), True)
                    link(v.max_index(top_i[:, k, :], top[:, k, :], lg[:, k, :]), True)
                link(v.tensor_copy(top_f[:], top_i[:]))
                v.tensor_tensor(pw[:, 0, :], top[:, :, 1], top[:, :, 0], ALU.subtract).then_inc(s["m_ex_in"], 1)
                v.wait_ge(s["m_ex_out"], j + 1)
                link(v.tensor_scalar(pw[:, 0, :], pw[:, 1, :], 1.0, None, ALU.add))
                link(v.reciprocal(pw[:, 2, :], pw[:, 0, :]))
                link(v.tensor_tensor(pw[:, 3, :], pw[:, 1, :], pw[:, 2, :], ALU.mult))
                iota = gate_rows[:, 2, :].unsqueeze(1).to_broadcast([P, GROUP, 8])
                for dst, k in ((comb, 0), (comb2, 1)):
                    link(v.tensor_tensor(dst[:], iota, top_f[:, :, k:k + 1].to_broadcast([P, GROUP, 8]),
                                         ALU.is_equal))
                    link(v.tensor_tensor(dst[:], dst[:], pw[:, 2 + k, :].unsqueeze(2).to_broadcast([P, GROUP, 8]),
                                         ALU.mult))
                v.tensor_tensor(comb[:], comb[:], comb2[:], ALU.add).then_inc(s["m_comb"], 1)
                assert link.n == M_LINKS
                link = Chain(v, s["e_chain"], j * E_LINKS)
                v.wait_ge(s["m_comb"], j + 1)
                for k in range(GROUP):
                    xt = x[:, ds(j * GROUP + k, 1), :].rearrange("p a f -> p (a f)")
                    for b in range(3):
                        n = k * 3 + b
                        v.wait_ge(s["e_y"], j * 12 + (n + 1))
                        bank = psum[:, 5 + n % 3, :]
                        for q in range(4 if b < 2 else 1):
                            y = bank[:, q * P:(q + 1) * P]
                            last = b == 2 or q == 3
                            if b < 2:
                                w = comb[:, k, b * 4 + q:b * 4 + q + 1]
                                ins = v.scalar_tensor_tensor(xt, y, w, xt, ALU.mult, ALU.add)
                            else:
                                ins = v.tensor_tensor(xt, xt, y, ALU.add)
                            if last:
                                ins.then_inc(s["e_used"], 1)
                                v.wait_ge(s["e_used"], j * 12 + (n + 1))
                            else:
                                link(ins)
                assert link.n == E_LINKS

        @block.scalar
        def _(a):
            a.wait_ge(s["rs_in"], 1)
            a.activation(st[:, 2, :], st[:, 1, :], ACT.Sqrt).then_inc(s["rs_out"], 1)
            a.wait_ge(s["rs_in"], 2)
            a.activation(st[:, 2, :], deg[:], ACT.Sqrt).then_inc(s["rs_out"], 1)
            with a.Fori(0, GROUPS) as j:
                a.wait_ge(s["msg_done"], j * 4 + 4)
                a.activation(msg_t[:, 0, :], psum[:, 0, :], ACT.Copy).then_inc(s["msg_a"], 1)
                a.wait_ge(s["gate_in"], j + 1)
                a.activation(small[:, 3, :], small[:, 2, :], ACT.Sigmoid, bias=b_att).then_inc(s["gate_out"], 1)
                a.wait_ge(s["rs_in"], j + 3)
                a.activation(small[:, 6, :], small[:, 5, :], ACT.Sqrt).then_inc(s["rs_out"], 1)
                a.wait_ge(s["xt_done"], j + 1)
                a.activation(xn_t[:, ds(j * GW, GW)], psum[:, 4, :], ACT.Copy).then_inc(s["xt_out"], 1)

            a.wait_ge(s["setup"], 2)
            with a.Fori(0, N // BODY) as i:
                a.activation(tables[:], neg_one[:], ACT.Sigmoid)
                for k in range(BODY):
                    t1 = i * BODY + (k + 1)
                    gates = gates_of[:, k % 2, :]
                    gate_g = psum[:, 4 + 2 * (k % 2), 0:1]
                    bank = k // STEPS % 2
                    c = k % STEPS
                    a.wait_ge(s["scan_zg"], t1)
                    a.activation(gate_g, psum[:, 2 + bank, c:c + 1], ACT.Tanh)
                    a.wait_ge(s["scan_z"], t1)
                    a.activation(gates, psum[:, bank, c:c + STEPS + 1:STEPS], ACT.Sigmoid).then_inc(s["scan_io"], 1)
                    a.wait_ge(s["scan_io"], t1)
                    a.wait_ge(s["scan_hc"], t1)
                    a.activation(psum[:, 5, 0:1], gate_g, ACT.Tanh, bias=hc[:, 0:1], scale=gates[:, 0:1]
                                 ).then_inc(s["scan_t"], 1)

            a.wait_ge(s["scaled"], 1)
            with a.Fori(0, GROUPS) as j:
                a.wait_ge(s["p_rs_in"], j + 1)
                a.activation(small[:, 6, :], small[:, 5, :], ACT.Sqrt).then_inc(s["p_rs_out"], 1)
                a.wait_ge(s["p_xt"], j + 1)
                a.activation(prep_t, psum[:, 1, :], ACT.Copy).then_inc(s["p_xt_out"], 1)
                for h in range(2 * HEADS):
                    a.wait_ge(s["p_qk"], j * 8 + h + 1)
                    if h > 1:
                        a.wait_ge(s["p_split"], j * 4 * HEADS + 2 * (h - 1))
                    a.activation(prep_qk[:, h % 2, :], psum[:, 3 + h % 2, :], ACT.Identity,
                                 bias=cols[:, 2 + h:3 + h], scale=SCALE if h < HEADS else 1.0
                                 ).then_inc(s["p_qk32"], 1)

            def evacuate_a(u, g):
                a.wait_ge(s["tp_done"], u * UT + g + 1)
                wait_past(a, s["pv_done"], u * UT, g - 3)
                a.activation(p_t[:, g % 4, :], psum[:, 4 + g % 2, :], ACT.Copy).then_inc(s["ev_act"], 1)

            def exponent(u, half, h):
                a.wait_ge(s["nm_done"], u * HEADS + h + 1)
                sc = score[:, half, h, :]
                a.activation(sc, sc, ACT.Exp, bias=nmx[:, half, h:h + 1], accum_out=lsum[:, half, h:h + 1]
                             ).then_inc(s["exp_done"], 1)

            def outputs_a(u):
                a.wait_ge(s["pv_done"], (u + 1) * UT)
                wait_past(a, s["y_done"], u, 0)
                a.activation(o_t[:], psum[:, 6, 0:P], ACT.Copy).then_inc(s["o_out"], 1)

            def keep_y0(u, t):
                wait_past(a, s["tile_done"], t, 0)
                a.wait_ge(s["y_done"], u + 1)
                a.activation(y0[:], psum[:, 7, :], ACT.Copy).then_inc(s["y0_out"], 1)

            def factors_a(t):
                a.wait_ge(s["fac_in"], t + 1)
                a.activation(fac[:, 2, :], fac[:, 1, :], ACT.Exp).then_inc(s["fac_out"], 1)

            def unit_a(t, half, before):
                u = t * 2 + half
                if half == 0 and before:
                    factors_a(t - 1)
                for h in range(HEADS):
                    if h:
                        exponent(u, half, h - 1)
                    if before or half:
                        for g in range(4 * h, 4 * h + 4):
                            if g not in V_ALL:
                                evacuate_a(u - 1, g)
                if before or half:
                    outputs_a(u - 1)
                exponent(u, half, HEADS - 1)
                if half:
                    keep_y0(u - 1, t)

            for half in range(2):
                unit_a(0, half, False)
            with a.Fori(1, TILES) as t:
                for half in range(2):
                    unit_a(t, half, True)
            factors_a(TILES - 1)
            for g in range(UT):
                if g not in V_ALL:
                    evacuate_a(2 * TILES - 1, g)
            outputs_a(2 * TILES - 1)

            with a.Fori(0, GROUPS) as j:
                a.wait_ge(s["m_rs_in"], j + 1)
                a.activation(small[:, 6, :], small[:, 5, :], ACT.Sqrt).then_inc(s["m_rs_out"], 1)
                a.wait_ge(s["m_xt"], j + 1)
                a.activation(xe_t, psum[:, 0, :], ACT.Copy).then_inc(s["m_xt_out"], 1)
                a.wait_ge(s["m_ex_in"], j + 1)
                a.activation(pw[:, 1, :], pw[:, 0, :], ACT.Exp).then_inc(s["m_ex_out"], 1)
                for k in range(HT):
                    a.wait_ge(s["e_h"], j * HT + k + 1)
                    a.activation(hid_t[:, k, :], psum[:, 2 + k % 3, :], ACT.Relu, bias=e_b1[:, k:k + 1]
                                 ).then_inc(s["e_hid"], 1)
                a.wait_ge(s["m_ct"], j + 1)
                a.activation(comb_t[:], psum[0:EXPERTS, 1, :], ACT.Copy).then_inc(s["m_ct_out"], 1)

        @block.tensor
        def _(pe):
            pe.wait_ge(s["consts_in"], 16 * len(consts))
            pe.wait_ge(s["setup"], 1)
            with pe.Fori(0, GROUPS) as j:
                for k in range(4):
                    pe.wait_ge(s["adj_t_in_%d" % k], (j + 1) * 16)
                    for b in range(8):
                        m = 8 * k + b
                        for f in range(2):
                            mm = pe.matmul(psum[:, f, :], feat[:, m, f * P:(f + 1) * P],
                                           stage[:, k, b * GW:(b + 1) * GW], start=(m == 0), stop=(m == TILES - 1))
                    mm.then_inc(s["msg_done"], 1)
                pe.wait_ge(s["msg_a"], j + 1)
                pe.wait_ge(s["msg_v"], j + 1)
                for f in range(2):
                    for t in range(GROUP):
                        mm = pe.matmul(psum[:, 2 + f, t * P:(t + 1) * P], msg_t[:, f, t * P:(t + 1) * P],
                                       gcn_w[:, f, :], start=True, stop=True)
                mm.then_inc(s["h_done"], 1)
                pe.wait_ge(s["ln_done"], j + 1)
                for t in range(GROUP):
                    mm = pe.transpose(psum[:, 4, t * P:(t + 1) * P], nrm[:, t, :], ident[:])
                mm.then_inc(s["xt_done"], 1)

            def gate_sums(bank, g):
                return psum[:, bank, g * STEPS:(g + 1) * STEPS] if g < 2 else psum[:, 2 + bank, 0:STEPS]

            def inputs_of(bank, at, k):
                g = k // 2
                dst = gate_sums(bank, g)
                if k % 2 == 0:
                    pe.matmul(dst, scan_u[:, g, :], xn_t[:, ds(at, STEPS)], start=(g != 1), stop=False,
                              skip_group_check=True)
                else:
                    pe.matmul(dst, scan_b[:, g, :], ones[:], start=False, stop=False, skip_group_check=True)

            pe.wait_ge(s["setup"], 2)
            pe.wait_ge(s["xt_out"], GROUPS)
            for k in range(6):
                inputs_of(0, 0, k)
            with pe.Fori(0, N // BODY) as i:
                for k in range(BODY):
                    b, c = k // STEPS % 2, k % STEPS
                    acc = [gate_sums(b, g)[:, c:c + 1] for g in range(3)]
                    pe.wait_ge(s["scan_hi"], i * BODY + (k + 1))
                    for part in (v_lo, v_hi):
                        for g in range(3):
                            pe.matmul(acc[g], part[:, g, :], h_hi[:], start=False, stop=False,
                                      skip_group_check=True)
                    pe.wait_ge(s["scan_lo"], i * BODY + (k + 1))
                    for g, signal in ((2, "scan_zg"), (0, None), (1, "scan_z")):
                        mm = pe.matmul(acc[g], v_hi[:, g, :], h_lo[:], start=False, stop=False,
                                       skip_group_check=True)
                        if signal:
                            mm.then_inc(s[signal], 1)
                    if c < 6:
                        inputs_of(1 - b, i * BODY + (k // STEPS + 1) * STEPS, c)

            pe.wait_ge(s["scan_kept"], N // BODY)
            pe.wait_ge(s["prepw_in"], 16)
            with pe.Fori(0, GROUPS) as j:
                pe.wait_ge(s["ht_in"], j + 1)
                for t in range(GROUP):
                    mm = pe.transpose(psum[:, 0, t * P:(t + 1) * P], h_stage[:, t * P:(t + 1) * P], ident[:])
                mm.then_inc(s["ht_done"], 1)
                pe.wait_ge(s["p_ln"], j + 1)
                for t in range(GROUP):
                    mm = pe.transpose(psum[:, 1, t * P:(t + 1) * P], nrm[:, t, :], ident[:])
                mm.then_inc(s["p_xt"], 1)
                pe.wait_ge(s["p_xt_out"], j + 1)
                for t in range(GROUP):
                    mm = pe.matmul(psum[:, 2, t * P:(t + 1) * P], prep_t[:, t * P:(t + 1) * P],
                                   prep_w[:, 2 * HEADS, :], start=True, stop=True)
                mm.then_inc(s["p_v"], 1)
                for h in range(2 * HEADS):
                    if h > 1:
                        pe.wait_ge(s["p_qk32"], j * 8 + (h - 1))
                    pe.matmul(psum[:, 3 + h % 2, :], prep_w[:, h, :], prep_t, start=True, stop=True
                              ).then_inc(s["p_qk"], 1)

            def scores(u, t, half, h, q):
                n = 8 * half + 2 * h + q
                wait_past(pe, s["ttr_done"], t * 16, n - 1)
                for c in range(2):
                    at = half * HALF + q * PAIR + c * 512
                    mm = pe.matmul(psum[:, 2 * q + c, :], q_st[:, h, ds(t * P, P)], k_st[:, h, at:at + 512],
                                   start=True, stop=True)
                mm.then_inc(s["qk_done"], 1)

            def transposes(u, half, g):
                if g == 0:
                    pe.wait_ge(s["exp_done"], (u + 1) * HEADS)
                if g >= 2:
                    wait_evacuated(pe, u, g - 2)
                elif not isinstance(u, int) or u > 0:
                    wait_evacuated(pe, u - 1, UT + g - 2)
                for h in range(HEADS):
                    mm = pe.transpose(psum[:, 4 + g % 2, h * P:(h + 1) * P],
                                      score[:, half, h, g * P:(g + 1) * P], ident[:])
                mm.then_inc(s["tp_done"], 1)

            def values(u, half, g):
                if g == 0:
                    wait_past(pe, s["o_out"], u, 0)
                wait_evacuated(pe, u, g)
                for h in range(HEADS):
                    mm = pe.matmul(psum[h * HD:(h + 1) * HD, 6, 0:P],
                                   v_nat[:, half * UT + g, h * HD:(h + 1) * HD],
                                   p_t[:, g % 4, h * P:(h + 1) * P], start=(g == 0), stop=(g == UT - 1),
                                   skip_group_check=True)
                mm.then_inc(s["pv_done"], 1)

            def project(u, t, half):
                pe.wait_ge(s["o_out"], u + 1)
                if half:
                    pe.wait_ge(s["y0_out"], t + 1)
                else:
                    wait_past(pe, s["tile_done"], t, 0)
                pe.matmul(psum[:, 7, :], o_t[:], w_out[:], start=True, stop=True).then_inc(s["y_done"], 1)

            def groups(u, half, gs):
                for g in gs:
                    transposes(u, half, g)
                    if g >= 2:
                        values(u, half, g - 2)

            def finish(u, t, half):
                for g in (UT - 2, UT - 1):
                    values(u, half, g)
                project(u, t, half)

            def unit_pe(t, half, before):
                u = t * 2 + half
                for h in range(HEADS):
                    scores(u, t, half, h, 0)
                    if h == 0:
                        scores(u, t, half, h, 1)
                    if before or half:
                        groups(u - 1, 1 - half, range(4 * h, 4 * h + 2))
                    if h:
                        scores(u, t, half, h, 1)
                    if before or half:
                        groups(u - 1, 1 - half, range(4 * h + 2, 4 * h + 4))
                if before or half:
                    finish(u - 1, t if half else t - 1, 1 - half)

            pe.wait_ge(s["p_split"], GROUPS * 4 * HEADS)
            pe.wait_ge(s["p_v_out"], GROUPS)
            for half in range(2):
                unit_pe(0, half, False)
            with pe.Fori(1, TILES) as t:
                for half in range(2):
                    unit_pe(t, half, True)
            groups(2 * TILES - 1, 1, range(UT))
            finish(2 * TILES - 1, TILES - 1, 1)

            pe.wait_ge(s["expw_in"], 32)
            with pe.Fori(0, GROUPS) as j:
                pe.wait_ge(s["m_ln"], j + 1)
                for t in range(GROUP):
                    mm = pe.transpose(psum[:, 0, t * P:(t + 1) * P], e_wrk[:, t, :], ident[:])
                mm.then_inc(s["m_xt"], 1)
                pe.wait_ge(s["m_xt_out"], j + 1)
                for t in range(GROUP):
                    mm = pe.matmul(psum[:, 1, t * EXPERTS:(t + 1) * EXPERTS], xe_t[:, t * P:(t + 1) * P],
                                   e_wg[:], start=True, stop=True)
                mm.then_inc(s["m_lg"], 1)
                for k in range(HT):
                    if k > 2:
                        pe.wait_ge(s["e_hid"], j * HT + (k - 2))
                    pe.matmul(psum[:, 2 + k % 3, :], e_w1[:, k * P:(k + 1) * P], xe_t,
                              start=True, stop=True).then_inc(s["e_h"], 1)
                pe.wait_ge(s["m_comb"], j + 1)
                for t in range(GROUP):
                    mm = pe.transpose(psum[0:EXPERTS, 1, t * P:(t + 1) * P], comb[:, t, :], ident[:])
                mm.then_inc(s["m_ct"], 1)
                pe.wait_ge(s["e_hid"], (j + 1) * HT)
                pe.wait_ge(s["m_ct_out"], j + 1)
                for k in range(GROUP):
                    rows_k = slice(k * P, (k + 1) * P)
                    for b in range(3):
                        n = k * 3 + b
                        if n > 2:
                            pe.wait_ge(s["e_used"], j * 3 * GROUP + (n - 2))
                        if b == 2:
                            mm = pe.matmul(psum[:, 5 + n % 3, 0:P], comb_t[:, rows_k], e_b2[:],
                                           start=True, stop=True)
                        else:
                            for q in range(4):
                                for i in range(2):
                                    m = 2 * (4 * b + q) + i
                                    mm = pe.matmul(psum[:, 5 + n % 3, q * P:(q + 1) * P], hid_t[:, m, rows_k],
                                                   e_w2[:, m, :], start=(i == 0), stop=(i == 1))
                        mm.then_inc(s["e_y"], 1)


def kernel(x, adj, L0_gnn_spatial_x, L0_gnn_W_f, L0_gnn_b_f, L0_gnn_W_s, L0_gnn_b_s, L0_gnn_W_att,
           L0_gnn_b_att, L0_ffn_U_i, L0_ffn_V_i, L0_ffn_b_i, L0_ffn_U_f, L0_ffn_V_f, L0_ffn_b_f,
           L0_ffn_U_c, L0_ffn_V_c, L0_ffn_b_c, L0_ffn_U_o, L0_ffn_V_o, L0_ffn_b_o, L1_gnn_Wqkv,
           L1_gnn_bqkv, L1_gnn_Wout, L1_gnn_bout, L1_gnn_graph_bias, L1_ffn_Wg, L1_ffn_bg,
           L1_ffn_bias, L1_ffn_W1, L1_ffn_b1, L1_ffn_W2, L1_ffn_b2):
    import concourse.bacc as bacc
    from concourse.bass_utils import run_bass_kernel_spmd

    def on_rows(v):
        return np.broadcast_to(np.asarray(v).reshape(1, -1), (P, v.size))

    def per_head(w):
        return [np.tile(w[..., h * HD:(h + 1) * HD], 4) for h in range(HEADS)]

    x, adj, wqkv, bqkv = (np.asarray(v) for v in (x, adj, L1_gnn_Wqkv, L1_gnn_bqkv))
    w_att, w_o = np.asarray(L0_gnn_W_att), np.asarray(L1_gnn_Wout)
    w_out = np.zeros((P, HEADS, P), np.float32)
    for h in range(HEADS):
        w_out[h * HD:(h + 1) * HD, h] = w_o[h * HD:(h + 1) * HD]
    arrays = {
        "x": x, "spatial": np.asarray(L0_gnn_spatial_x), "adj": adj, "adj_t": np.ascontiguousarray(adj.T),
        "ident": np.eye(P, dtype=np.float32),
        "rows": np.stack([on_rows(v) for v in (L0_gnn_b_f, L0_gnn_b_s, w_att[:P], w_att[P:], L1_gnn_bout,
                                               bqkv[2 * P:])], 1),
        "gcn_w": np.stack([L0_gnn_W_f, L0_gnn_W_s], 1),
        "cols": np.concatenate([on_rows(np.asarray(L0_gnn_b_att)), on_rows(np.asarray(L1_gnn_graph_bias)),
                                np.stack(per_head(bqkv[:P]) + per_head(bqkv[P:2 * P]), 1)], 1),
        "gate_rows": np.stack([on_rows(np.asarray(v)) for v in (L1_ffn_bg, L1_ffn_bias,
                                                                np.arange(EXPERTS, dtype=np.float32))], 1),
        "scan_v": np.stack([L0_ffn_V_i, L0_ffn_V_o, L0_ffn_V_c], 1),
        "scan_u": np.stack([L0_ffn_U_i, L0_ffn_U_o, L0_ffn_U_c], 1),
        "scan_b": np.stack([L0_ffn_b_i, L0_ffn_b_o, L0_ffn_b_c])[None],
        "w_out": w_out.reshape(P, HEADS * P),
        "qkv_w": np.stack(per_head(wqkv[:, :P]) + per_head(wqkv[:, P:2 * P]) + [wqkv[:, 2 * P:]], 1),
        "e_w1": np.transpose(L1_ffn_W1, (1, 0, 2)).reshape(P, EXPERTS * HID),
        "e_w2": np.transpose(np.asarray(L1_ffn_W2).reshape(HT, P, P), (1, 0, 2)),
        "e_b1": np.asarray(L1_ffn_b1).reshape(HT, P).T,
        "e_b2": np.asarray(L1_ffn_b2),
        "e_wg": np.asarray(L1_ffn_Wg),
    }
    arrays = {k: np.ascontiguousarray(v) for k, v in arrays.items()}
    nc = bacc.Bacc("TRN2", target_bir_lowering=False, num_devices=1)
    d = {k: nc.dram_tensor("in_" + k, v.shape, F32, kind="ExternalInput").ap() for k, v in arrays.items()}
    out = nc.dram_tensor("out", (N, P), F32, kind="ExternalOutput").ap()
    build(nc, d, out)
    return run_bass_kernel_spmd(nc, [{"in_" + k: v for k, v in arrays.items()}], core_ids=[0]).results[0]["out"]
```

```python
from contextlib import ExitStack

import numpy as np

import concourse.bass as bass
from concourse import mybir
from concourse.bass import ds

F32 = mybir.dt.float32
F16 = mybir.dt.float16
U32 = mybir.dt.uint32
ALU = mybir.AluOpType
ACT = mybir.ActivationFunctionType
AX_X = mybir.AxisListType.X

P = 128
N = 4096
TILES = N // P
GROUP = 4
GROUPS = TILES // GROUP
GW = GROUP * P
EPS = 1e-5
DEG_EPS = 1e-9
MASKED = -1e9
HEADS = 4
HD = P // HEADS
SCALE = HD ** -0.5
EXPERTS = 8
HID = 256
HT = EXPERTS * HID // P
STEPS = 16
BODY = 4 * STEPS
HALF = N // 2
UT = HALF // P
PAIR = 1024


def wait_apart(eng, signal, value):
    reg = eng.to_reg(value)
    eng.wait_ge(signal, 0)
    eng.wait_ge(signal, reg)

G_LINKS, P_LINKS, M_LINKS, E_LINKS = 24, 11, 28, 24


class Chain:

    def __init__(self, eng, sem, base=0):
        self.eng, self.sem, self.base, self.n = eng, sem, base, 0

    def __call__(self, ins, apart=False):
        self.n += 1
        ins.then_inc(self.sem, 1)
        if apart:
            wait_apart(self.eng, self.sem, self.base + self.n)
        else:
            self.eng.wait_ge(self.sem, self.base + self.n)


def build(nc, d, out):
    ctx = ExitStack()
    with ctx:
        def sb(name, shape, dt=F32):
            return ctx.enter_context(nc.sbuf_tensor(name, shape, dt))

        def sem(name):
            return ctx.enter_context(nc.semaphore(name))

        x = sb("x", [P, TILES, P])
        ident = sb("ident", [P, P])
        rows = sb("rows", [P, 6, P])
        gcn_w = sb("gcn_w", [P, 2, P])
        cols = sb("cols", [P, 10])
        gate_rows = sb("gate_rows", [P, 3, 8])
        scan_b = sb("scan_b", [1, 3, P])
        w_out = sb("w_out", [P, HEADS * P])
        e_b1 = sb("e_b1", [P, HT])
        e_b2 = sb("e_b2", [EXPERTS, P])
        e_wg = sb("e_wg", [P, EXPERTS])
        arena = sb("arena", [P, 43008])
        psum = ctx.enter_context(nc.psum_tensor("psum", [P, 8, 512], F32))
        b_f, b_s, wa_f, wa_s, b_out, b_v = (rows[:, k, :] for k in range(6))
        b_att, g_bias = cols[:, 0:1], cols[:, 1:2]

        def view(at, shape, dt=F32):
            n = int(np.prod(shape)) // (2 if dt == F16 else 1)
            ap = arena[:, at:at + n]
            if dt == F16:
                ap = ap.bitcast(F16)
            if len(shape) == 2:
                ap = ap.rearrange("p (a b) -> p a b", a=shape[0])
            if len(shape) == 3:
                ap = ap.rearrange("p (a b c) -> p a b c", a=shape[0], b=shape[1])
            return ap

        stage = view(0, [4, N])
        feat = view(16384, [TILES, 2 * P])
        hs_t = view(20480, [N])
        xn_t = view(24576, [N + BODY])
        msg_t = view(28736, [2, GW])
        cen = view(29760, [GROUP, P])
        hs_g = view(30272, [GROUP, P])
        wrk = view(30784, [GROUP, P])
        nrm = view(31296, [GROUP, P])
        scan_v = view(31808, [3, P])
        scan_u = view(32192, [3, P])
        v_res = view(32576, [3, P])
        v_hi = view(32960, [3, P], F16)
        v_lo = view(33152, [3, P], F16)
        v_nat = view(0, [TILES, P])
        q_st = view(4096, [HEADS, N], F16)
        k_st = view(12288, [HEADS, N], F16)
        prep_t = view(28736, [GW])
        h_stage = view(29248, [GW])
        prep_qk = view(32576, [2, GW])
        prep_w = view(36864, [2 * HEADS + 1, P])
        score = view(20480, [2, HEADS, HALF])
        bias_a = view(36864, [2, HALF])
        p_t = view(40960, [4, GW])
        mask = sb("mask", [P, 2, 512])
        o_t = sb("o_t", [P, P])
        y0 = sb("y0", [P, HEADS * P])
        e_w1 = view(0, [EXPERTS * HID])
        e_w2 = view(2048, [HT, P])
        xe_t = view(4096, [GW])
        e_cen = view(4608, [GROUP, P])
        e_wrk = view(5120, [GROUP, P])
        hid_t = view(8192, [HT, GW])
        deg = sb("deg", [P, TILES])
        dinv = sb("dinv", [P, TILES])
        st = sb("st", [P, 4, TILES])
        small = sb("small", [P, 8, GROUP])
        ones = sb("ones", [1, STEPS])
        neg_one = sb("neg_one", [P, 1])
        h_hi = sb("h_hi", [P, 1], F16)
        h_lo = sb("h_lo", [P, 1], F16)
        hc = sb("hc", [P, 1])
        cell = sb("cell", [P, 1])
        h_new = sb("h_new", [P, BODY])
        tables = sb("tables", [P, 1])
        gates_of = sb("gates", [P, 2, 2])
        mx = sb("mx", [P, HEADS, 2])
        nmx = sb("nmx", [P, 2, HEADS])
        lsum = sb("lsum", [P, 2, HEADS])
        fac = sb("fac", [P, 6, 2 * HEADS])
        lg = sb("lg", [P, GROUP, 8])
        top = sb("top", [P, GROUP, 8])
        top_i = sb("top_i", [P, GROUP, 8], U32)
        top_f = sb("top_f", [P, GROUP, 8])
        pw = sb("pw", [P, 4, GROUP])
        comb = sb("comb", [P, GROUP, EXPERTS])
        comb2 = sb("comb2", [P, GROUP, EXPERTS])
        comb_t = sb("comb_t", [EXPERTS, GW])

        names = """consts_in x_in adj_in_0 adj_in_1 adj_in_2 adj_in_3 adj_summed
        adj_t_in_0 adj_t_in_1 adj_t_in_2 adj_t_in_3 msg_done msg_a msg_v h_done
        gate_in gate_out rs_in rs_out ln_done xt_done xt_out g_chain s_chain s2_chain
        setup scan_z scan_zg scan_kept scan_io scan_t scan_hi scan_lo scan_h scan_hc
        ht_in ht_done p_rs_in p_rs_out p_ln p_xt p_xt_out p_qk p_qk32 p_hi p_split p_v p_v_out p_chain scaled
        prepw_in bias_in_0 bias_in_1 masked bias_ready qk_done ttr_done nm_done exp_done tp_done ev_act ev_dve pv_done
        o_out y_done y0_out y_used fac_in fac_out f_chain c_chain tile_done
        m_rs_in m_rs_out m_ln m_xt m_xt_out m_lg m_ex_in m_ex_out m_comb m_ct m_ct_out m_chain
        expw_in e_h e_hid e_y e_used e_chain stored""".split()
        s = {k: sem(k) for k in names}

        block = ctx.enter_context(nc.Block())

        x_rows = d["x"].rearrange("(t p) f -> p t f", p=P)
        sp_rows = d["spatial"].rearrange("(t p) f -> p t f", p=P)
        adj_rows = d["adj"].rearrange("(t p) m -> p t m", p=P)
        adj_t = d["adj_t"].rearrange("(b p) n -> p b n", p=P)
        out_rows = out.rearrange("(t p) f -> p t f", p=P)
        consts = ((ident[:], "ident"), (rows[:], "rows"), (gcn_w[:], "gcn_w"), (cols[:], "cols"),
                  (gate_rows[:], "gate_rows"), (scan_b[:], "scan_b"), (scan_v, "scan_v"), (scan_u, "scan_u"),
                  (w_out[:], "w_out"), (e_b1[:], "e_b1"), (e_b2[:], "e_b2"), (e_wg[:], "e_wg"))

        def over_rows(row):
            return row.unsqueeze(1).to_broadcast([P, GROUP, P])

        def over_cols(col, n=GROUP, w=P):
            return col.unsqueeze(2).to_broadcast([P, n, w])

        def tiles_of(bank):
            return psum[:, bank, :].rearrange("p (t f) -> p t f", f=P)

        V_TILES = (4, 8, 12)

        def wait_past(eng, signal, base, more):
            if not isinstance(base, int) or base + more > 0:
                eng.wait_ge(signal, base + more)

        def wait_evacuated(eng, n_unit, g):
            if g in V_TILES:
                eng.wait_ge(s["ev_dve"], n_unit * len(V_TILES) + V_TILES.index(g) + 1)
            else:
                mine = [k for k in range(UT) if k not in V_TILES]
                eng.wait_ge(s["ev_act"], n_unit * len(mine) + mine.index(g) + 1)

        @block.sync
        def _(e):
            e.dma_start(x[:], x_rows).then_inc(s["x_in"], 16)
            e.dma_start(feat[:, :, P:2 * P], sp_rows).then_inc(s["x_in"], 16)
            for dst, src in consts:
                e.dma_start(dst, d[src]).then_inc(s["consts_in"], 16)
            for k in range(4):
                e.dma_start(stage[:, k, :], adj_rows[:, k, :]).then_inc(s["adj_in_%d" % k], 16)
            with e.Fori(1, TILES // 4) as i:
                for k in range(4):
                    e.wait_ge(s["adj_summed"], i * 4 + (k - 3))
                    e.dma_start(stage[:, k, :].unsqueeze(1), adj_rows[:, ds(i * 4 + k, 1), :]
                                ).then_inc(s["adj_in_%d" % k], 16)
            for k in range(4):
                e.wait_ge(s["adj_summed"], TILES - 3 + k)
                e.dma_start(stage[:, k, :].rearrange("p (b n) -> p b n", b=8),
                            adj_t[:, 8 * k:8 * k + 8, 0:GW]).then_inc(s["adj_t_in_%d" % k], 16)
            with e.Fori(1, GROUPS) as j:
                for k in range(4):
                    e.wait_ge(s["msg_done"], j * 4 + (k - 3))
                    e.dma_start(stage[:, k, :].rearrange("p (b n) -> p b n", b=8),
                                adj_t[:, 8 * k:8 * k + 8, ds(j * GW, GW)]).then_inc(s["adj_t_in_%d" % k], 16)
            e.wait_ge(s["setup"], 2)
            e.dma_start(prep_w, d["qkv_w"]).then_inc(s["prepw_in"], 16)
            e.wait_ge(s["p_qk"], GROUPS * 2 * HEADS)
            e.wait_ge(s["p_v"], GROUPS)
            for k in range(2):
                e.dma_start(bias_a[:, k, :], adj_rows[:, 0, k * HALF:(k + 1) * HALF]).then_inc(s["bias_in_%d" % k], 16)
            with e.Fori(1, TILES) as t:
                for k in range(2):
                    e.wait_ge(s["ttr_done"], t * 16 + (k - 1) * 8)
                    e.dma_start(bias_a[:, k, :].unsqueeze(1),
                                adj_rows[:, ds(t, 1), k * HALF:(k + 1) * HALF]).then_inc(s["bias_in_%d" % k], 16)
            e.wait_ge(s["pv_done"], 2 * TILES * UT)
            e.dma_start(e_w1, d["e_w1"]).then_inc(s["expw_in"], 16)
            e.dma_start(e_w2, d["e_w2"]).then_inc(s["expw_in"], 16)
            with e.Fori(0, GROUPS) as j:
                e.wait_ge(s["e_used"], (j + 1) * 3 * GROUP)
                e.dma_start(out_rows[:, ds(j * GROUP, GROUP), :], x[:, ds(j * GROUP, GROUP), :]
                            ).then_inc(s["stored"], 16)
            e.wait_ge(s["stored"], 16 * GROUPS)

        def centre(v, link, src, dst, tmp, mean, var, ready):
            link(v.tensor_reduce(mean, src, AX_X, ALU.add))
            link(v.tensor_scalar(mean, mean, 1.0 / P, None, ALU.mult))
            link(v.tensor_tensor(dst, src, over_cols(mean, dst.shape[1]), ALU.subtract))
            link(v.tensor_tensor(tmp, dst, dst, ALU.mult))
            link(v.tensor_reduce(var, tmp, AX_X, ALU.add))
            v.tensor_scalar(var, var, 1.0 / P, EPS, ALU.mult, ALU.add).then_inc(ready, 1)

        def rsqrt(v, link, a, root, r, t):
            link(v.reciprocal(r, root))
            link(v.tensor_tensor(t, r, r, ALU.mult))
            link(v.tensor_tensor(t, t, a, ALU.mult))
            link(v.tensor_scalar(t, t, -0.5, 1.5, ALU.mult, ALU.add))
            link(v.tensor_tensor(r, r, t, ALU.mult))

        @block.vector
        def _(v):
            link = Chain(v, s["s_chain"])
            v.wait_ge(s["x_in"], 32)
            v.wait_ge(s["consts_in"], 16 * len(consts))
            centre(v, link, x[:], feat[:, :, 0:P], xn_t[:, 0:N].rearrange("p (t f) -> p t f", f=P),
                   st[:, 0, :], st[:, 1, :], s["rs_in"])
            v.wait_ge(s["rs_out"], 1)
            rsqrt(v, link, st[:, 1, :], st[:, 2, :], st[:, 3, :], st[:, 0, :])
            link(v.tensor_tensor(feat[:, :, 0:P], feat[:, :, 0:P], over_cols(st[:, 3, :], TILES), ALU.mult))
            with v.Fori(0, TILES // 4) as i:
                for k in range(4):
                    wait_apart(v, s["adj_in_%d" % k], (i + 1) * 16)
                    v.tensor_reduce(deg[:, ds(i * 4 + k, 1)], stage[:, k, :], AX_X, ALU.add
                                    ).then_inc(s["adj_summed"], 1)
            link = Chain(v, s["s2_chain"])
            v.wait_ge(s["adj_summed"], TILES)
            v.tensor_scalar(deg[:], deg[:], DEG_EPS, None, ALU.add).then_inc(s["rs_in"], 1)
            v.wait_ge(s["rs_out"], 2)
            rsqrt(v, link, deg[:], st[:, 2, :], dinv[:], st[:, 0, :])
            v.tensor_tensor(feat, feat, over_cols(dinv[:], TILES, 2 * P), ALU.mult).then_inc(s["setup"], 1)
            link(v.tensor_copy(v_hi, scan_v))
            link(v.tensor_tensor(v_res, scan_v, v_hi, ALU.subtract))
            link(v.tensor_copy(v_lo, v_res))
            link(v.memset(ones[:], 1.0))
            link(v.memset(xn_t[:, N:], 0.0))
            v.memset(hc[:], 0.0).then_inc(s["scan_hc"], 1)
            v.memset(h_hi[:], 0.0).then_inc(s["scan_hi"], 1)
            v.memset(h_lo[:], 0.0).then_inc(s["scan_lo"], 1)
            v.memset(neg_one[:], -1.0).then_inc(s["setup"], 1)

            hf = cen
            with v.Fori(0, GROUPS) as j:
                link = Chain(v, s["g_chain"], j * G_LINKS)
                xg = x[:, ds(j * GROUP, GROUP), :]
                dg = over_cols(dinv[:, ds(j * GROUP, GROUP)])
                v.wait_ge(s["msg_done"], j * 4 + 4)
                v.tensor_copy(msg_t[:, 1, :], psum[:, 1, :]).then_inc(s["msg_v"], 1)
                v.wait_ge(s["h_done"], j + 1)
                for h, bank, bias in ((hf, 2, b_f), (hs_g, 3, b_s)):
                    link(v.tensor_tensor(h, tiles_of(bank), dg, ALU.mult))
                    link(v.tensor_tensor(h, h, over_rows(bias), ALU.add))
                    link(v.tensor_scalar(h, h, 0.0, None, ALU.max))
                for k, h, w in ((0, hf, wa_f), (1, hs_g, wa_s)):
                    link(v.tensor_tensor(wrk, h, over_rows(w), ALU.mult))
                    link(v.tensor_reduce(small[:, k, :], wrk, AX_X, ALU.add))
                v.tensor_tensor(small[:, 2, :], small[:, 0, :], small[:, 1, :], ALU.add).then_inc(s["gate_in"], 1)
                link(v.tensor_tensor(hf, hf, hs_g, ALU.subtract))
                link(v.tensor_tensor(xg, xg, hs_g, ALU.add))
                v.wait_ge(s["gate_out"], j + 1)
                link(v.tensor_tensor(hf, hf, over_cols(small[:, 3, :]), ALU.mult))
                link(v.tensor_tensor(xg, xg, hf, ALU.add), True)
                centre(v, link, xg, cen, wrk, small[:, 4, :], small[:, 5, :], s["rs_in"])
                v.wait_ge(s["rs_out"], j + 3)
                rsqrt(v, link, small[:, 5, :], small[:, 6, :], small[:, 7, :], small[:, 4, :])
                v.tensor_tensor(nrm, cen, over_cols(small[:, 7, :]), ALU.mult).then_inc(s["ln_done"], 1)
                assert link.n == G_LINKS

            v.wait_ge(s["ln_done"], GROUPS)
            with v.Fori(0, N // BODY) as i:
                for k in range(BODY):
                    t1 = i * BODY + (k + 1)
                    tanh_c, gates, h_k = psum[:, 5, 0:1], gates_of[:, k % 2, :], h_new[:, k:k + 1]
                    v.wait_ge(s["scan_t"], t1)
                    v.tensor_tensor(h_hi[:], gates[:, 1:2], tanh_c, ALU.mult).then_inc(s["scan_hi"], 1)
                    v.wait_ge(s["scan_hi"], t1 + 1)
                    v.scalar_tensor_tensor(h_lo[:], tanh_c, gates[:, 1:2], h_hi[:], ALU.mult, ALU.subtract
                                           ).then_inc(s["scan_lo"], 1)
                    v.scalar_tensor_tensor(cell[:], psum[:, 4 + 2 * (k % 2), 0:1], gates[:, 0:1], hc[:],
                                           ALU.mult, ALU.add)
                    v.tensor_tensor(h_k, gates[:, 1:2], tanh_c, ALU.mult).then_inc(s["scan_h"], 1)
                    v.wait_ge(s["scan_h"], t1)
                    v.tensor_tensor(hc[:], h_k, cell[:], ALU.mult).then_inc(s["scan_hc"], 1)
                v.tensor_copy(hs_t[:, ds(i * BODY, BODY)], h_new[:]).then_inc(s["scan_kept"], 1)

            v.wait_ge(s["scan_kept"], N // BODY)
            v.tensor_scalar(cols[:, 2:6], cols[:, 2:6], SCALE, None, ALU.mult).then_inc(s["scaled"], 1)
            with v.Fori(0, GROUPS) as j:
                link = Chain(v, s["p_chain"], j * P_LINKS)
                xg = x[:, ds(j * GROUP, GROUP), :]
                v.tensor_copy(h_stage, hs_t[:, ds(j * GW, GW)]).then_inc(s["ht_in"], 1)
                v.wait_ge(s["ht_done"], j + 1)
                link(v.tensor_tensor(xg, xg, tiles_of(0), ALU.add), True)
                centre(v, link, xg, cen, wrk, small[:, 4, :], small[:, 5, :], s["p_rs_in"])
                v.wait_ge(s["p_rs_out"], j + 1)
                rsqrt(v, link, small[:, 5, :], small[:, 6, :], small[:, 7, :], small[:, 4, :])
                v.tensor_tensor(nrm, cen, over_cols(small[:, 7, :]), ALU.mult).then_inc(s["p_ln"], 1)
                v.wait_ge(s["p_v"], j + 1)
                v.tensor_tensor(v_nat[:, ds(j * GROUP, GROUP), :], tiles_of(2), over_rows(b_v), ALU.add
                                ).then_inc(s["p_v_out"], 1)
                for h in range(2 * HEADS):
                    dst = (q_st if h < HEADS else k_st)[:, h % HEADS, ds(j * GW, GW)]
                    src = prep_qk[:, h % 2, :]
                    v.wait_ge(s["p_qk32"], j * 8 + h + 1)
                    v.tensor_copy(dst, src).then_inc(s["p_hi"], 1)
                    v.wait_ge(s["p_hi"], j * 8 + h + 1)
                    if h < HEADS:
                        v.tensor_tensor(dst[64:128], src[64:128], dst[64:128], ALU.subtract
                                        ).then_inc(s["p_split"], 2)
                    else:
                        for q in (32, 96):
                            v.tensor_tensor(dst[q:q + 32], src[q:q + 32], dst[q:q + 32], ALU.subtract
                                            ).then_inc(s["p_split"], 1)
                assert link.n == P_LINKS

            def bias_quarter(t, half, q):
                u = 2 * t + half
                c = bias_a[:, half, q * 512:(q + 1) * 512]
                v.wait_ge(s["masked"], u * 4 + q + 1)
                v.scalar_tensor_tensor(c, c, g_bias, mask[:, q % 2, :], ALU.mult, ALU.add
                                       ).then_inc(s["bias_ready"], 1)

            def evacuate_v(u, g):
                v.wait_ge(s["tp_done"], u * UT + g + 1)
                wait_past(v, s["pv_done"], u * UT, g - 3)
                v.tensor_copy(p_t[:, g % 4, :], psum[:, 4 + g % 2, :]).then_inc(s["ev_dve"], 1)

            def factors_in(t):
                link = Chain(v, s["f_chain"], t * 6)
                m0, m1 = nmx[:, 0, :], nmx[:, 1, :]
                link(v.tensor_tensor(fac[:, 0, 0:4], m0, m1, ALU.min))
                link(v.tensor_tensor(fac[:, 1, 0:4], fac[:, 0, 0:4], m0, ALU.subtract))
                v.tensor_tensor(fac[:, 1, 4:8], fac[:, 0, 0:4], m1, ALU.subtract).then_inc(s["fac_in"], 1)
                return link

            def factors_out(t, link):
                v.wait_ge(s["fac_out"], t + 1)
                link(v.tensor_tensor(fac[:, 3, :], fac[:, 2, :], lsum[:].rearrange("p a h -> p (a h)"), ALU.mult))
                link(v.tensor_tensor(fac[:, 4, 0:4], fac[:, 3, 0:4], fac[:, 3, 4:8], ALU.add))
                link(v.reciprocal(fac[:, 4, 4:8], fac[:, 4, 0:4]))
                link(v.tensor_tensor(fac[:, 5, :].rearrange("p (a h) -> p a h", a=2),
                                     fac[:, 2, :].rearrange("p (a h) -> p a h", a=2),
                                     fac[:, 4, 4:8].unsqueeze(1).to_broadcast([P, 2, HEADS]), ALU.mult))
                assert link.n == 6, link.n

            def combine(t, k):
                xt = x[:, ds(t, 1), :].rearrange("p a f -> p (a f)")
                if k:
                    v.wait_ge(s["c_chain"], t * 8 + k)
                if k == 0:
                    ins = v.tensor_tensor(xt, xt, b_out, ALU.add)
                else:
                    if k == 1:
                        v.wait_ge(s["y0_out"], t + 1)
                    if k == 5:
                        v.wait_ge(s["y_done"], 2 * t + 2)
                    h = (k - 1) % HEADS
                    y = y0[:, h * P:(h + 1) * P] if k < 5 else psum[:, 7, h * P:(h + 1) * P]
                    ins = v.scalar_tensor_tensor(xt, y, fac[:, 5, k - 1:k], xt, ALU.mult, ALU.add)
                ins.then_inc(s["c_chain" if k < 8 else "tile_done"], 1)

            def unit_v(t, half, before, after):
                u = t * 2 + half
                v.wait_ge(s["bias_ready"], (u + 1) * 4)
                for h in range(HEADS):
                    for q in range(2):
                        n = u * 8 + 2 * h + q
                        c = slice(q * PAIR, (q + 1) * PAIR)
                        if h == 0 and q == 0 and before:
                            v.wait_ge(s["tp_done"], (u - 1) * UT)
                        wait_apart(v, s["qk_done"], n + 1)
                        v.tensor_tensor_reduce(score[:, half, h, c].rearrange("p (a b) -> p a b", a=2),
                                               psum[:, 2 * q:2 * q + 2, :],
                                               bias_a[:, half, c].rearrange("p (a b) -> p a b", a=2),
                                               1.0, -3e38, ALU.add, ALU.max, mx[:, h, q:q + 1]
                                               ).then_inc(s["ttr_done"], 1)
                        if h and q == 0 and (before or half):
                            evacuate_v(u - 1, V_TILES[h - 1])
                        if h and half and before:
                            combine(t - 1, 3 * (h - 1) + q)
                    if h == 0 and half == 0 and before:
                        v.wait_ge(s["exp_done"], u * HEADS)
                        factors_out(t - 1, factors_in(t - 1))
                    v.wait_ge(s["ttr_done"], u * 8 + 2 * h + 2)
                    v.scalar_tensor_tensor(nmx[:, half, h:h + 1], mx[:, h, 0:1], mx[:, h, 1:2], neg_one[:],
                                           ALU.max, ALU.mult).then_inc(s["nm_done"], 1)
                    if after or not half:
                        bias_quarter(t + half, 1 - half, h)
                    if h and half and before:
                        combine(t - 1, 3 * (h - 1) + 2)

            v.wait_ge(s["p_split"], GROUPS * 2 * 2 * HEADS)
            for q in range(4):
                bias_quarter(0, 0, q)
            for half in range(2):
                unit_v(0, half, False, True)
            with v.Fori(1, TILES - 1) as t:
                for half in range(2):
                    unit_v(t, half, True, True)
            for half in range(2):
                unit_v(TILES - 1, half, True, False)
            v.wait_ge(s["exp_done"], 2 * TILES * HEADS)
            factors_out(TILES - 1, factors_in(TILES - 1))
            for g in V_TILES:
                evacuate_v(2 * TILES - 1, g)
            for k in range(9):
                combine(TILES - 1, k)

            v.wait_ge(s["tile_done"], TILES)
            with v.Fori(0, GROUPS) as j:
                link = Chain(v, s["m_chain"], j * M_LINKS)
                xg = x[:, ds(j * GROUP, GROUP), :]
                centre(v, link, xg, e_cen, e_wrk, small[:, 4, :], small[:, 5, :], s["m_rs_in"])
                v.wait_ge(s["m_rs_out"], j + 1)
                rsqrt(v, link, small[:, 5, :], small[:, 6, :], small[:, 7, :], small[:, 4, :])
                v.tensor_tensor(e_wrk, e_cen, over_cols(small[:, 7, :]), ALU.mult).then_inc(s["m_ln"], 1)
                v.wait_ge(s["m_lg"], j + 1)
                for k in range(2):
                    acc = psum[:, 1, 0:GROUP * 8].rearrange("p (t f) -> p t f", f=8)
                    link(v.tensor_tensor(lg[:], lg[:] if k else acc,
                                         gate_rows[:, k, :].unsqueeze(1).to_broadcast([P, GROUP, 8]), ALU.add),
                         k == 1)
                for k in range(GROUP):
                    link(v.max(top[:, k, :], lg[:, k, :]), True)
                    link(v.max_index(top_i[:, k, :], top[:, k, :], lg[:, k, :]), True)
                link(v.tensor_copy(top_f[:], top_i[:]))
                v.tensor_tensor(pw[:, 0, :], top[:, :, 1], top[:, :, 0], ALU.subtract).then_inc(s["m_ex_in"], 1)
                v.wait_ge(s["m_ex_out"], j + 1)
                link(v.tensor_scalar(pw[:, 0, :], pw[:, 1, :], 1.0, None, ALU.add))
                link(v.reciprocal(pw[:, 2, :], pw[:, 0, :]))
                link(v.tensor_tensor(pw[:, 3, :], pw[:, 1, :], pw[:, 2, :], ALU.mult))
                iota = gate_rows[:, 2, :].unsqueeze(1).to_broadcast([P, GROUP, 8])
                for dst, k in ((comb, 0), (comb2, 1)):
                    link(v.tensor_tensor(dst[:], iota, top_f[:, :, k:k + 1].to_broadcast([P, GROUP, 8]),
                                         ALU.is_equal))
                    link(v.tensor_tensor(dst[:], dst[:], pw[:, 2 + k, :].unsqueeze(2).to_broadcast([P, GROUP, 8]),
                                         ALU.mult))
                v.tensor_tensor(comb[:], comb[:], comb2[:], ALU.add).then_inc(s["m_comb"], 1)
                assert link.n == M_LINKS
                link = Chain(v, s["e_chain"], j * E_LINKS)
                v.wait_ge(s["m_comb"], j + 1)
                for k in range(GROUP):
                    xt = x[:, ds(j * GROUP + k, 1), :].rearrange("p a f -> p (a f)")
                    for b in range(3):
                        n = k * 3 + b
                        v.wait_ge(s["e_y"], j * 12 + (n + 1))
                        bank = psum[:, 5 + n % 3, :]
                        for q in range(4 if b < 2 else 1):
                            y = bank[:, q * P:(q + 1) * P]
                            last = b == 2 or q == 3
                            if b < 2:
                                w = comb[:, k, b * 4 + q:b * 4 + q + 1]
                                ins = v.scalar_tensor_tensor(xt, y, w, xt, ALU.mult, ALU.add)
                            else:
                                ins = v.tensor_tensor(xt, xt, y, ALU.add)
                            if last:
                                ins.then_inc(s["e_used"], 1)
                                v.wait_ge(s["e_used"], j * 12 + (n + 1))
                            else:
                                link(ins)
                assert link.n == E_LINKS

        @block.gpsimd
        def _(g):
            def mask_unit(t, half):
                for q in range(4):
                    n = 4 * half + q
                    if q == 0:
                        wait_apart(g, s["bias_in_%d" % half], (t + 1) * 16)
                    if isinstance(t, int) and t == 0:
                        if n > 1:
                            g.wait_ge(s["bias_ready"], n - 1)
                    else:
                        wait_apart(g, s["bias_ready"], t * 8 + (n - 1))
                    g.tensor_scalar(mask[:, q % 2, :], bias_a[:, half, q * 512:(q + 1) * 512], 0.0, MASKED,
                                    ALU.is_equal, ALU.mult).then_inc(s["masked"], 1)

            g.wait_ge(s["setup"], 2)
            for half in range(2):
                mask_unit(0, half)
            with g.Fori(1, TILES) as t:
                for half in range(2):
                    mask_unit(t, half)

        @block.scalar
        def _(a):
            a.wait_ge(s["rs_in"], 1)
            a.activation(st[:, 2, :], st[:, 1, :], ACT.Sqrt).then_inc(s["rs_out"], 1)
            a.wait_ge(s["rs_in"], 2)
            a.activation(st[:, 2, :], deg[:], ACT.Sqrt).then_inc(s["rs_out"], 1)
            with a.Fori(0, GROUPS) as j:
                a.wait_ge(s["msg_done"], j * 4 + 4)
                a.activation(msg_t[:, 0, :], psum[:, 0, :], ACT.Copy).then_inc(s["msg_a"], 1)
                a.wait_ge(s["gate_in"], j + 1)
                a.activation(small[:, 3, :], small[:, 2, :], ACT.Sigmoid, bias=b_att).then_inc(s["gate_out"], 1)
                a.wait_ge(s["rs_in"], j + 3)
                a.activation(small[:, 6, :], small[:, 5, :], ACT.Sqrt).then_inc(s["rs_out"], 1)
                a.wait_ge(s["xt_done"], j + 1)
                a.activation(xn_t[:, ds(j * GW, GW)], psum[:, 4, :], ACT.Copy).then_inc(s["xt_out"], 1)

            a.wait_ge(s["setup"], 2)
            with a.Fori(0, N // BODY) as i:
                a.activation(tables[:], neg_one[:], ACT.Sigmoid)
                for k in range(BODY):
                    t1 = i * BODY + (k + 1)
                    gates = gates_of[:, k % 2, :]
                    gate_g = psum[:, 4 + 2 * (k % 2), 0:1]
                    bank = k // STEPS % 2
                    c = k % STEPS
                    a.wait_ge(s["scan_zg"], t1)
                    a.activation(gate_g, psum[:, 2 + bank, c:c + 1], ACT.Tanh)
                    a.wait_ge(s["scan_z"], t1)
                    a.activation(gates, psum[:, bank, c:c + STEPS + 1:STEPS], ACT.Sigmoid).then_inc(s["scan_io"], 1)
                    a.wait_ge(s["scan_io"], t1)
                    a.wait_ge(s["scan_hc"], t1)
                    a.activation(psum[:, 5, 0:1], gate_g, ACT.Tanh, bias=hc[:, 0:1], scale=gates[:, 0:1]
                                 ).then_inc(s["scan_t"], 1)

            a.wait_ge(s["scaled"], 1)
            with a.Fori(0, GROUPS) as j:
                a.wait_ge(s["p_rs_in"], j + 1)
                a.activation(small[:, 6, :], small[:, 5, :], ACT.Sqrt).then_inc(s["p_rs_out"], 1)
                a.wait_ge(s["p_xt"], j + 1)
                a.activation(prep_t, psum[:, 1, :], ACT.Copy).then_inc(s["p_xt_out"], 1)
                for h in range(2 * HEADS):
                    a.wait_ge(s["p_qk"], j * 8 + h + 1)
                    if h > 1:
                        a.wait_ge(s["p_split"], j * 4 * HEADS + 2 * (h - 1))
                    a.activation(prep_qk[:, h % 2, :], psum[:, 3 + h % 2, :], ACT.Identity,
                                 bias=cols[:, 2 + h:3 + h], scale=SCALE if h < HEADS else 1.0
                                 ).then_inc(s["p_qk32"], 1)

            def evacuate_a(u, g):
                a.wait_ge(s["tp_done"], u * UT + g + 1)
                wait_past(a, s["pv_done"], u * UT, g - 3)
                a.activation(p_t[:, g % 4, :], psum[:, 4 + g % 2, :], ACT.Copy).then_inc(s["ev_act"], 1)

            def exponent(u, half, h):
                a.wait_ge(s["nm_done"], u * HEADS + h + 1)
                sc = score[:, half, h, :]
                a.activation(sc, sc, ACT.Exp, bias=nmx[:, half, h:h + 1], accum_out=lsum[:, half, h:h + 1]
                             ).then_inc(s["exp_done"], 1)

            def outputs_a(u):
                a.wait_ge(s["pv_done"], (u + 1) * UT)
                wait_past(a, s["y_done"], u, 0)
                a.activation(o_t[:], psum[:, 6, 0:P], ACT.Copy).then_inc(s["o_out"], 1)

            def keep_y0(u, t):
                wait_past(a, s["tile_done"], t, 0)
                a.wait_ge(s["y_done"], u + 1)
                a.activation(y0[:], psum[:, 7, :], ACT.Copy).then_inc(s["y0_out"], 1)

            def factors_a(t):
                a.wait_ge(s["fac_in"], t + 1)
                a.activation(fac[:, 2, :], fac[:, 1, :], ACT.Exp).then_inc(s["fac_out"], 1)

            def first_slot_a(t, half, done):
                u = t * 2 + half
                exponent(u - 1, 1 - half, HEADS - 1)
                if done:
                    outputs_a(u - 2)
                for g in (0, 1):
                    evacuate_a(u - 1, g)
                if half == 0:
                    factors_a(t - 1)
                if half == 0 and done:
                    keep_y0(u - 2, t - 1)
                for g in (2, 3):
                    evacuate_a(u - 1, g)

            def unit_a(t, half, before):
                u = t * 2 + half
                if before or half:
                    first_slot_a(t, half, before)
                for h in range(1, HEADS):
                    exponent(u, half, h - 1)
                    if before or half:
                        for g in range(4 * h, 4 * h + 4):
                            if g not in V_TILES:
                                evacuate_a(u - 1, g)

            for half in range(2):
                unit_a(0, half, False)
            with a.Fori(1, TILES) as t:
                for half in range(2):
                    unit_a(t, half, True)
            first_slot_a(TILES, 0, True)
            for g in range(4, UT):
                if g not in V_TILES:
                    evacuate_a(2 * TILES - 1, g)
            outputs_a(2 * TILES - 1)

            with a.Fori(0, GROUPS) as j:
                a.wait_ge(s["m_rs_in"], j + 1)
                a.activation(small[:, 6, :], small[:, 5, :], ACT.Sqrt).then_inc(s["m_rs_out"], 1)
                a.wait_ge(s["m_xt"], j + 1)
                a.activation(xe_t, psum[:, 0, :], ACT.Copy).then_inc(s["m_xt_out"], 1)
                a.wait_ge(s["m_ex_in"], j + 1)
                a.activation(pw[:, 1, :], pw[:, 0, :], ACT.Exp).then_inc(s["m_ex_out"], 1)
                for k in range(HT):
                    a.wait_ge(s["e_h"], j * HT + k + 1)
                    a.activation(hid_t[:, k, :], psum[:, 2 + k % 3, :], ACT.Relu, bias=e_b1[:, k:k + 1]
                                 ).then_inc(s["e_hid"], 1)
                a.wait_ge(s["m_ct"], j + 1)
                a.activation(comb_t[:], psum[0:EXPERTS, 1, :], ACT.Copy).then_inc(s["m_ct_out"], 1)

        @block.tensor
        def _(pe):
            pe.wait_ge(s["consts_in"], 16 * len(consts))
            pe.wait_ge(s["setup"], 1)
            with pe.Fori(0, GROUPS) as j:
                for k in range(4):
                    pe.wait_ge(s["adj_t_in_%d" % k], (j + 1) * 16)
                    for b in range(8):
                        m = 8 * k + b
                        for f in range(2):
                            mm = pe.matmul(psum[:, f, :], feat[:, m, f * P:(f + 1) * P],
                                           stage[:, k, b * GW:(b + 1) * GW], start=(m == 0), stop=(m == TILES - 1))
                    mm.then_inc(s["msg_done"], 1)
                pe.wait_ge(s["msg_a"], j + 1)
                pe.wait_ge(s["msg_v"], j + 1)
                for f in range(2):
                    for t in range(GROUP):
                        mm = pe.matmul(psum[:, 2 + f, t * P:(t + 1) * P], msg_t[:, f, t * P:(t + 1) * P],
                                       gcn_w[:, f, :], start=True, stop=True)
                mm.then_inc(s["h_done"], 1)
                pe.wait_ge(s["ln_done"], j + 1)
                for t in range(GROUP):
                    mm = pe.transpose(psum[:, 4, t * P:(t + 1) * P], nrm[:, t, :], ident[:])
                mm.then_inc(s["xt_done"], 1)

            def gate_sums(bank, g):
                return psum[:, bank, g * STEPS:(g + 1) * STEPS] if g < 2 else psum[:, 2 + bank, 0:STEPS]

            def inputs_of(bank, at, k):
                g = k // 2
                dst = gate_sums(bank, g)
                if k % 2 == 0:
                    pe.matmul(dst, scan_u[:, g, :], xn_t[:, ds(at, STEPS)], start=(g != 1), stop=False,
                              skip_group_check=True)
                else:
                    pe.matmul(dst, scan_b[:, g, :], ones[:], start=False, stop=False, skip_group_check=True)

            pe.wait_ge(s["setup"], 2)
            pe.wait_ge(s["xt_out"], GROUPS)
            for k in range(6):
                inputs_of(0, 0, k)
            with pe.Fori(0, N // BODY) as i:
                for k in range(BODY):
                    b, c = k // STEPS % 2, k % STEPS
                    acc = [gate_sums(b, g)[:, c:c + 1] for g in range(3)]
                    pe.wait_ge(s["scan_hi"], i * BODY + (k + 1))
                    for part in (v_lo, v_hi):
                        for g in range(3):
                            pe.matmul(acc[g], part[:, g, :], h_hi[:], start=False, stop=False,
                                      skip_group_check=True)
                    pe.wait_ge(s["scan_lo"], i * BODY + (k + 1))
                    for g, signal in ((2, "scan_zg"), (0, None), (1, "scan_z")):
                        mm = pe.matmul(acc[g], v_hi[:, g, :], h_lo[:], start=False, stop=False,
                                       skip_group_check=True)
                        if signal:
                            mm.then_inc(s[signal], 1)
                    if c < 6:
                        inputs_of(1 - b, i * BODY + (k // STEPS + 1) * STEPS, c)

            pe.wait_ge(s["scan_kept"], N // BODY)
            pe.wait_ge(s["prepw_in"], 16)
            with pe.Fori(0, GROUPS) as j:
                pe.wait_ge(s["ht_in"], j + 1)
                for t in range(GROUP):
                    mm = pe.transpose(psum[:, 0, t * P:(t + 1) * P], h_stage[:, t * P:(t + 1) * P], ident[:])
                mm.then_inc(s["ht_done"], 1)
                pe.wait_ge(s["p_ln"], j + 1)
                for t in range(GROUP):
                    mm = pe.transpose(psum[:, 1, t * P:(t + 1) * P], nrm[:, t, :], ident[:])
                mm.then_inc(s["p_xt"], 1)
                pe.wait_ge(s["p_xt_out"], j + 1)
                for t in range(GROUP):
                    mm = pe.matmul(psum[:, 2, t * P:(t + 1) * P], prep_t[:, t * P:(t + 1) * P],
                                   prep_w[:, 2 * HEADS, :], start=True, stop=True)
                mm.then_inc(s["p_v"], 1)
                for h in range(2 * HEADS):
                    if h > 1:
                        pe.wait_ge(s["p_qk32"], j * 8 + (h - 1))
                    pe.matmul(psum[:, 3 + h % 2, :], prep_w[:, h, :], prep_t, start=True, stop=True
                              ).then_inc(s["p_qk"], 1)

            def scores(u, t, half, h, q):
                n = 8 * half + 2 * h + q
                wait_past(pe, s["ttr_done"], t * 16, n - 1)
                for c in range(2):
                    at = half * HALF + q * PAIR + c * 512
                    mm = pe.matmul(psum[:, 2 * q + c, :], q_st[:, h, ds(t * P, P)], k_st[:, h, at:at + 512],
                                   start=True, stop=True)
                mm.then_inc(s["qk_done"], 1)

            def transposes(u, half, g):
                if g == 0:
                    pe.wait_ge(s["exp_done"], (u + 1) * HEADS)
                if g >= 2:
                    wait_evacuated(pe, u, g - 2)
                elif not isinstance(u, int) or u > 0:
                    wait_evacuated(pe, u - 1, UT + g - 2)
                for h in range(HEADS):
                    mm = pe.transpose(psum[:, 4 + g % 2, h * P:(h + 1) * P],
                                      score[:, half, h, g * P:(g + 1) * P], ident[:])
                mm.then_inc(s["tp_done"], 1)

            def values(u, half, g):
                if g == 0:
                    wait_past(pe, s["o_out"], u, 0)
                wait_evacuated(pe, u, g)
                for h in range(HEADS):
                    mm = pe.matmul(psum[h * HD:(h + 1) * HD, 6, 0:P],
                                   v_nat[:, half * UT + g, h * HD:(h + 1) * HD],
                                   p_t[:, g % 4, h * P:(h + 1) * P], start=(g == 0), stop=(g == UT - 1),
                                   skip_group_check=True)
                mm.then_inc(s["pv_done"], 1)

            def project(u, t, half):
                pe.wait_ge(s["o_out"], u + 1)
                if half:
                    pe.wait_ge(s["y0_out"], t + 1)
                else:
                    wait_past(pe, s["tile_done"], t, 0)
                pe.matmul(psum[:, 7, :], o_t[:], w_out[:], start=True, stop=True).then_inc(s["y_done"], 1)

            def column(u, half, g):
                transposes(u, half, g)
                if g >= 2:
                    values(u, half, g - 2)

            def unit_pe(t, half, before, after):
                u = t * 2 + half
                w, w_half = u - 1, 1 - half
                for h in range(HEADS):
                    nxt = (u, t, half, h + 1)
                    if h == HEADS - 1:
                        nxt = (u + 1, t + half, 1 - half, 0)
                    last = h == HEADS - 1 and half and not after
                    if h == 0 and before:
                        values(u - 2, half, UT - 2)
                        values(u - 2, half, UT - 1)
                    if before or half:
                        column(w, w_half, 4 * h)
                        if h:
                            column(w, w_half, 4 * h + 1)
                    if not last:
                        scores(*nxt, 0)
                    if before or half:
                        column(w, w_half, 4 * h + (2 if h else 1))
                        if h == HEADS - 1:
                            column(w, w_half, 4 * h + 3)
                    if not last:
                        scores(*nxt, 1)
                    if h == 0 and before:
                        project(u - 2, t - 1, half)
                    if before or half:
                        if h == 0:
                            column(w, w_half, 2)
                        if h < HEADS - 1:
                            column(w, w_half, 4 * h + 3)

            pe.wait_ge(s["p_split"], GROUPS * 4 * HEADS)
            pe.wait_ge(s["p_v_out"], GROUPS)
            for q in range(2):
                scores(0, 0, 0, 0, q)
            for half in range(2):
                unit_pe(0, half, False, True)
            with pe.Fori(1, TILES - 1) as t:
                for half in range(2):
                    unit_pe(t, half, True, True)
            for half in range(2):
                unit_pe(TILES - 1, half, True, False)
            last = 2 * TILES - 1
            values(last - 1, 0, UT - 2)
            values(last - 1, 0, UT - 1)
            column(last, 1, 0)
            column(last, 1, 1)
            project(last - 1, TILES - 1, 0)
            for g in range(2, UT):
                column(last, 1, g)
            values(last, 1, UT - 2)
            values(last, 1, UT - 1)
            project(last, TILES - 1, 1)

            pe.wait_ge(s["expw_in"], 32)
            with pe.Fori(0, GROUPS) as j:
                pe.wait_ge(s["m_ln"], j + 1)
                for t in range(GROUP):
                    mm = pe.transpose(psum[:, 0, t * P:(t + 1) * P], e_wrk[:, t, :], ident[:])
                mm.then_inc(s["m_xt"], 1)
                pe.wait_ge(s["m_xt_out"], j + 1)
                for t in range(GROUP):
                    mm = pe.matmul(psum[:, 1, t * EXPERTS:(t + 1) * EXPERTS], xe_t[:, t * P:(t + 1) * P],
                                   e_wg[:], start=True, stop=True)
                mm.then_inc(s["m_lg"], 1)
                for k in range(HT):
                    if k > 2:
                        pe.wait_ge(s["e_hid"], j * HT + (k - 2))
                    pe.matmul(psum[:, 2 + k % 3, :], e_w1[:, k * P:(k + 1) * P], xe_t,
                              start=True, stop=True).then_inc(s["e_h"], 1)
                pe.wait_ge(s["m_comb"], j + 1)
                for t in range(GROUP):
                    mm = pe.transpose(psum[0:EXPERTS, 1, t * P:(t + 1) * P], comb[:, t, :], ident[:])
                mm.then_inc(s["m_ct"], 1)
                pe.wait_ge(s["e_hid"], (j + 1) * HT)
                pe.wait_ge(s["m_ct_out"], j + 1)
                for k in range(GROUP):
                    rows_k = slice(k * P, (k + 1) * P)
                    for b in range(3):
                        n = k * 3 + b
                        if n > 2:
                            pe.wait_ge(s["e_used"], j * 3 * GROUP + (n - 2))
                        if b == 2:
                            mm = pe.matmul(psum[:, 5 + n % 3, 0:P], comb_t[:, rows_k], e_b2[:],
                                           start=True, stop=True)
                        else:
                            for q in range(4):
                                for i in range(2):
                                    m = 2 * (4 * b + q) + i
                                    mm = pe.matmul(psum[:, 5 + n % 3, q * P:(q + 1) * P], hid_t[:, m, rows_k],
                                                   e_w2[:, m, :], start=(i == 0), stop=(i == 1))
                        mm.then_inc(s["e_y"], 1)


def kernel(x, adj, L0_gnn_spatial_x, L0_gnn_W_f, L0_gnn_b_f, L0_gnn_W_s, L0_gnn_b_s, L0_gnn_W_att,
           L0_gnn_b_att, L0_ffn_U_i, L0_ffn_V_i, L0_ffn_b_i, L0_ffn_U_f, L0_ffn_V_f, L0_ffn_b_f,
           L0_ffn_U_c, L0_ffn_V_c, L0_ffn_b_c, L0_ffn_U_o, L0_ffn_V_o, L0_ffn_b_o, L1_gnn_Wqkv,
           L1_gnn_bqkv, L1_gnn_Wout, L1_gnn_bout, L1_gnn_graph_bias, L1_ffn_Wg, L1_ffn_bg,
           L1_ffn_bias, L1_ffn_W1, L1_ffn_b1, L1_ffn_W2, L1_ffn_b2):
    import concourse.bacc as bacc
    from concourse.bass_utils import run_bass_kernel_spmd

    def on_rows(v):
        return np.broadcast_to(np.asarray(v).reshape(1, -1), (P, v.size))

    def per_head(w):
        return [np.tile(w[..., h * HD:(h + 1) * HD], 4) for h in range(HEADS)]

    x, adj, wqkv, bqkv = (np.asarray(v) for v in (x, adj, L1_gnn_Wqkv, L1_gnn_bqkv))
    w_att, w_o = np.asarray(L0_gnn_W_att), np.asarray(L1_gnn_Wout)
    w_out = np.zeros((P, HEADS, P), np.float32)
    for h in range(HEADS):
        w_out[h * HD:(h + 1) * HD, h] = w_o[h * HD:(h + 1) * HD]
    arrays = {
        "x": x, "spatial": np.asarray(L0_gnn_spatial_x), "adj": adj, "adj_t": np.ascontiguousarray(adj.T),
        "ident": np.eye(P, dtype=np.float32),
        "rows": np.stack([on_rows(v) for v in (L0_gnn_b_f, L0_gnn_b_s, w_att[:P], w_att[P:], L1_gnn_bout,
                                               bqkv[2 * P:])], 1),
        "gcn_w": np.stack([L0_gnn_W_f, L0_gnn_W_s], 1),
        "cols": np.concatenate([on_rows(np.asarray(L0_gnn_b_att)), on_rows(np.asarray(L1_gnn_graph_bias)),
                                np.stack(per_head(bqkv[:P]) + per_head(bqkv[P:2 * P]), 1)], 1),
        "gate_rows": np.stack([on_rows(np.asarray(v)) for v in (L1_ffn_bg, L1_ffn_bias,
                                                                np.arange(EXPERTS, dtype=np.float32))], 1),
        "scan_v": np.stack([L0_ffn_V_i, L0_ffn_V_o, L0_ffn_V_c], 1),
        "scan_u": np.stack([L0_ffn_U_i, L0_ffn_U_o, L0_ffn_U_c], 1),
        "scan_b": np.stack([L0_ffn_b_i, L0_ffn_b_o, L0_ffn_b_c])[None],
        "w_out": w_out.reshape(P, HEADS * P),
        "qkv_w": np.stack(per_head(wqkv[:, :P]) + per_head(wqkv[:, P:2 * P]) + [wqkv[:, 2 * P:]], 1),
        "e_w1": np.transpose(L1_ffn_W1, (1, 0, 2)).reshape(P, EXPERTS * HID),
        "e_w2": np.transpose(np.asarray(L1_ffn_W2).reshape(HT, P, P), (1, 0, 2)),
        "e_b1": np.asarray(L1_ffn_b1).reshape(HT, P).T,
        "e_b2": np.asarray(L1_ffn_b2),
        "e_wg": np.asarray(L1_ffn_Wg),
    }
    arrays = {k: np.ascontiguousarray(v) for k, v in arrays.items()}
    nc = bacc.Bacc("TRN2", target_bir_lowering=False, num_devices=1)
    d = {k: nc.dram_tensor("in_" + k, v.shape, F32, kind="ExternalInput").ap() for k, v in arrays.items()}
    out = nc.dram_tensor("out", (N, P), F32, kind="ExternalOutput").ap()
    build(nc, d, out)
    return run_bass_kernel_spmd(nc, [{"in_" + k: v for k, v in arrays.items()}], core_ids=[0]).results[0]["out"]
```

```python
from contextlib import ExitStack

import numpy as np

import concourse.bass as bass
from concourse import mybir
from concourse.bass import ds

F32 = mybir.dt.float32
F16 = mybir.dt.float16
I32 = mybir.dt.int32
U32 = mybir.dt.uint32
ALU = mybir.AluOpType
ACT = mybir.ActivationFunctionType
AX_X = mybir.AxisListType.X

P = 128
N = 4096
TILES = N // P
GROUP = 4
GROUPS = TILES // GROUP
GW = GROUP * P
EPS = 1e-5
DEG_EPS = 1e-9
MASKED = -1e9
HEADS = 4
HD = P // HEADS
SCALE = HD ** -0.5
EXPERTS = 8
HID = 256
HT = EXPERTS * HID // P
STEPS = 16
BODY = P
HALF = N // 2
UT = HALF // P
PAIR = 1024
AHEAD = 2
AW = AHEAD * P
G_BODIES = TILES - AHEAD
G_LINKS, MN_LINKS, M_LINKS, E_LINKS = 24, 10, 18, 24
SG_LINKS, SP_LINKS = 27, 40
SG_LOGIT = 6
SP_V = 20


def wait_apart(eng, signal, value):
    reg = eng.to_reg(value)
    eng.wait_ge(signal, 0)
    eng.wait_ge(signal, reg)


class Chain:

    def __init__(self, eng, sem, base=0):
        self.eng, self.sem, self.base, self.n = eng, sem, base, 0

    def __call__(self, ins, apart=False):
        self.n += 1
        ins.then_inc(self.sem, 1)
        if apart:
            wait_apart(self.eng, self.sem, self.base + self.n)
        else:
            self.eng.wait_ge(self.sem, self.base + self.n)


class Steps:

    def __init__(self, eng, sem, base):
        self.eng, self.sem, self.base, self.n = eng, sem, base, 0

    def __call__(self, op, *args, apart=False, **kw):
        if self.n:
            if apart:
                wait_apart(self.eng, self.sem, self.base + self.n)
            else:
                self.eng.wait_ge(self.sem, self.base + self.n)
        self.n += 1
        return op(*args, **kw).then_inc(self.sem, 1)


def build(nc, d, out):
    ctx = ExitStack()
    with ctx:
        def sb(name, shape, dt=F32):
            return ctx.enter_context(nc.sbuf_tensor(name, shape, dt))

        def sem(name):
            return ctx.enter_context(nc.semaphore(name))

        x = sb("x", [P, TILES, P])
        ident = sb("ident", [P, P])
        rows = sb("rows", [P, 6, P])
        gcn_w = sb("gcn_w", [P, 2, P])
        cols = sb("cols", [P, 10])
        gate_rows = sb("gate_rows", [P, 3, 8])
        scan_b = sb("scan_b", [1, 3, P])
        w_out = sb("w_out", [P, HEADS * P])
        e_b1 = sb("e_b1", [P, HT])
        e_b2 = sb("e_b2", [EXPERTS, P])
        e_wg = sb("e_wg", [P, EXPERTS])
        arena = sb("arena", [P, 43008])
        psum = ctx.enter_context(nc.psum_tensor("psum", [P, 8, 512], F32))
        b_f, b_s, wa_f, wa_s, b_out, b_v = (rows[:, k, :] for k in range(6))
        b_att, g_bias = cols[:, 0:1], cols[:, 1:2]

        def view(at, shape, dt=F32):
            n = int(np.prod(shape)) // (2 if dt == F16 else 1)
            ap = arena[:, at:at + n]
            if dt == F16:
                ap = ap.bitcast(F16)
            if len(shape) == 2:
                ap = ap.rearrange("p (a b) -> p a b", a=shape[0])
            if len(shape) == 3:
                ap = ap.rearrange("p (a b c) -> p a b c", a=shape[0], b=shape[1])
            return ap

        stage = view(0, [4, N])
        feat = view(20480, [TILES, 2 * P])
        first_adj = [view(at, [8 * AW]) for at in (16384, 18432, 28672, 30720)]
        msg_t = view(33792, [2, AW])
        cen = view(34304, [AHEAD, P])
        hs_g = view(34560, [AHEAD, P])
        wrk = view(34816, [AHEAD, P])
        nrm = view(35072, [AHEAD, P])
        stage_s = view(28672, [N])
        xn_t = view(32768, [N + STEPS])
        prep_w = view(36880, [2 * HEADS + 1, P])
        prep_t = view(38032, [P])
        prep_qk = view(38160, [2, P])
        s_msg_t = view(38416, [2, P])
        s_h = view(38672, [2, P])
        s_wrk = view(38928, [2, P])
        s_cen = view(39184, [P])
        s_nrm = view(39312, [P])
        scan_v = view(39440, [3, P])
        scan_u = view(39824, [3, P])
        v_res = view(40208, [3, P])
        v_hi = view(40592, [3, P], F16)
        v_lo = view(40784, [3, P], F16)
        v_nat = view(0, [TILES, P])
        q_st = view(4096, [HEADS, N], F16)
        k_st = view(12288, [HEADS, N], F16)
        score = view(20480, [2, HEADS, HALF])
        bias_a = view(36864, [2, HALF])
        p_t = view(40960, [4, GW])
        mask = sb("mask", [P, 2, 512])
        o_t = sb("o_t", [P, P])
        y0 = sb("y0", [P, HEADS * P])
        e_w1 = view(0, [EXPERTS * HID])
        e_w2 = view(2048, [HT, P])
        xe_t = view(4096, [GW])
        e_cen = view(4608, [GROUP, P])
        e_wrk = view(5120, [GROUP, P])
        hid_t = view(8192, [HT, GW])
        deg = sb("deg", [P, TILES])
        dinv = sb("dinv", [P, TILES])
        st = sb("st", [P, 4, TILES])
        small = sb("small", [P, 8, GROUP])
        ones = sb("ones", [1, STEPS])
        neg_one = sb("neg_one", [P, 1])
        h_hi = sb("h_hi", [P, 1], F16)
        h_lo = sb("h_lo", [P, 1], F16)
        hc = sb("hc", [P, 1])
        cell = sb("cell", [P, 1])
        h_new = sb("h_new", [P, BODY])
        h_prev = sb("h_prev", [P, BODY])
        s_col = sb("s_col", [P, 12])
        tables = sb("tables", [P, 1])
        gates_of = sb("gates", [P, 2, 2])
        mx = sb("mx", [P, HEADS, 2])
        nmx = sb("nmx", [P, 2, HEADS])
        lsum = sb("lsum", [P, 2, HEADS])
        fac = sb("fac", [P, 6, 2 * HEADS])
        lg = sb("lg", [P, GROUP, 8])
        top = sb("top", [P, GROUP, 8])
        top_i = sb("top_i", [P, GROUP, 8], U32)
        top_f = sb("top_f", [P, GROUP, 8])
        pw = sb("pw", [P, 4, GROUP])
        comb = sb("comb", [P, GROUP, EXPERTS])
        comb2 = sb("comb2", [P, GROUP, EXPERTS])
        comb_t = sb("comb_t", [EXPERTS, GW])

        names = """consts_in x_in adj_in_0 adj_in_1 adj_in_2 adj_in_3 adj_summed
        adj_t_in_0 adj_t_in_1 adj_t_in_2 adj_t_in_3 msg_done msg_a msg_v h_done
        gate_in gate_out rs_in rs_out ln_done xt_done xt_out g_chain s_chain s2_chain
        setup scan_z scan_zg scan_kept scan_io scan_t scan_hi scan_lo scan_h scan_c scan_hc
        sg_adj_in sg_msg sg_msg_t sg_w sg_gate_out sg_xt sg_xt_out side_g
        sp_ht sp_xt sp_xt_out sp_v sp_qk sp_qk32 side_p scaled
        prepw_in bias_in_0 bias_in_1 masked bias_ready qk_done ttr_done nm_done exp_done
        tp_done ev_act ev_dve pv_done
        o_out y_done y0_out fac_in fac_out f_chain c_chain tile_done
        m_rs_in m_rs_out m_ln m_xt m_xt_out m_lg m_ex_in m_ex_out m_comb m_ct m_ct_out mn_chain m_chain
        expw_in e_h e_hid e_y e_used e_chain stored""".split()
        s = {k: sem(k) for k in names}

        block = ctx.enter_context(nc.Block())

        x_rows = d["x"].rearrange("(t p) f -> p t f", p=P)
        sp_rows = d["spatial"].rearrange("(t p) f -> p t f", p=P)
        adj_rows = d["adj"].rearrange("(t p) m -> p t m", p=P)
        adj_t = d["adj_t"].rearrange("(b p) n -> p b n", p=P)
        out_rows = out.rearrange("(t p) f -> p t f", p=P)
        consts = ((ident[:], "ident"), (rows[:], "rows"), (gcn_w[:], "gcn_w"), (cols[:], "cols"),
                  (gate_rows[:], "gate_rows"), (scan_b[:], "scan_b"), (scan_v, "scan_v"), (scan_u, "scan_u"),
                  (w_out[:], "w_out"), (e_b1[:], "e_b1"), (e_b2[:], "e_b2"), (e_wg[:], "e_wg"))

        def over_rows(row):
            return row.unsqueeze(1).to_broadcast([P, AHEAD, P])

        def over_cols(col, n=GROUP, w=P):
            return col.unsqueeze(2).to_broadcast([P, n, w])

        def tiles_of(bank):
            return psum[:, bank, :].rearrange("p (t f) -> p t f", f=P)

        V_TILES = (4, 8, 12)

        def wait_past(eng, signal, base, more):
            if not isinstance(base, int) or base + more > 0:
                eng.wait_ge(signal, base + more)

        def wait_evacuated(eng, n_unit, g):
            if g in V_TILES:
                eng.wait_ge(s["ev_dve"], n_unit * len(V_TILES) + V_TILES.index(g) + 1)
            else:
                mine = [k for k in range(UT) if k not in V_TILES]
                eng.wait_ge(s["ev_act"], n_unit * len(mine) + mine.index(g) + 1)

        @block.sync
        def _(e):
            e.dma_start(x[:], x_rows).then_inc(s["x_in"], 16)
            e.dma_start(feat[:, :, P:2 * P], sp_rows).then_inc(s["x_in"], 16)
            for dst, src in consts:
                e.dma_start(dst, d[src]).then_inc(s["consts_in"], 16)
            for k in range(4):
                e.dma_start(stage[:, k, :], adj_rows[:, k, :]).then_inc(s["adj_in_%d" % k], 16)
            with e.Fori(1, TILES // 4) as i:
                for k in range(4):
                    e.wait_ge(s["adj_summed"], i * 4 + (k - 3))
                    e.dma_start(stage[:, k, :].unsqueeze(1), adj_rows[:, ds(i * 4 + k, 1), :]
                                ).then_inc(s["adj_in_%d" % k], 16)
            for k in range(4):
                e.dma_start(first_adj[k].rearrange("p (b n) -> p b n", b=8), adj_t[:, 8 * k:8 * k + 8, 0:AW]
                            ).then_inc(s["adj_t_in_%d" % k], 16)
            e.dma_start(prep_w, d["qkv_w"]).then_inc(s["prepw_in"], 16)
            e.wait_ge(s["xt_done"], 1)
            e.dma_start(stage_s.rearrange("p (b n) -> p b n", b=TILES), adj_t[:, :, AHEAD * P:(AHEAD + 1) * P]
                        ).then_inc(s["sg_adj_in"], 16)
            with e.Fori(1, G_BODIES) as i:
                e.wait_ge(s["sg_msg"], i)
                e.dma_start(stage_s.rearrange("p (b n) -> p b n", b=TILES), adj_t[:, :, ds((i + AHEAD) * P, P)]
                            ).then_inc(s["sg_adj_in"], 16)
            e.wait_ge(s["side_p"], TILES * SP_LINKS)
            for k in range(2):
                e.dma_start(bias_a[:, k, :], adj_rows[:, 0, k * HALF:(k + 1) * HALF]).then_inc(s["bias_in_%d" % k], 16)
            with e.Fori(1, TILES) as t:
                for k in range(2):
                    e.wait_ge(s["ttr_done"], t * 16 + (k - 1) * 8)
                    e.dma_start(bias_a[:, k, :].unsqueeze(1),
                                adj_rows[:, ds(t, 1), k * HALF:(k + 1) * HALF]).then_inc(s["bias_in_%d" % k], 16)
            e.wait_ge(s["pv_done"], 2 * TILES * UT)
            e.dma_start(e_w1, d["e_w1"]).then_inc(s["expw_in"], 16)
            e.dma_start(e_w2, d["e_w2"]).then_inc(s["expw_in"], 16)
            with e.Fori(0, GROUPS) as j:
                e.wait_ge(s["e_used"], (j + 1) * 3 * GROUP)
                e.dma_start(out_rows[:, ds(j * GROUP, GROUP), :], x[:, ds(j * GROUP, GROUP), :]
                            ).then_inc(s["stored"], 16)
            e.wait_ge(s["stored"], 16 * GROUPS)

        def centre(v, link, src, dst, tmp, mean, var, ready):
            link(v.tensor_reduce(mean, src, AX_X, ALU.add))
            link(v.tensor_scalar(mean, mean, 1.0 / P, None, ALU.mult))
            link(v.tensor_tensor(dst, src, over_cols(mean, dst.shape[1]), ALU.subtract))
            link(v.tensor_tensor(tmp, dst, dst, ALU.mult))
            link(v.tensor_reduce(var, tmp, AX_X, ALU.add))
            v.tensor_scalar(var, var, 1.0 / P, EPS, ALU.mult, ALU.add).then_inc(ready, 1)

        def rsqrt(v, link, a, root, r, t):
            link(v.reciprocal(r, root))
            link(v.tensor_tensor(t, r, r, ALU.mult))
            link(v.tensor_tensor(t, t, a, ALU.mult))
            link(v.tensor_scalar(t, t, -0.5, 1.5, ALU.mult, ALU.add))
            link(v.tensor_tensor(r, r, t, ALU.mult))

        @block.vector
        def _(v):
            link = Chain(v, s["s_chain"])
            v.wait_ge(s["x_in"], 32)
            v.wait_ge(s["consts_in"], 16 * len(consts))
            centre(v, link, x[:], feat[:, :, 0:P], xn_t[:, 0:N].rearrange("p (t f) -> p t f", f=P),
                   st[:, 0, :], st[:, 1, :], s["rs_in"])
            v.wait_ge(s["rs_out"], 1)
            rsqrt(v, link, st[:, 1, :], st[:, 2, :], st[:, 3, :], st[:, 0, :])
            link(v.tensor_tensor(feat[:, :, 0:P], feat[:, :, 0:P], over_cols(st[:, 3, :], TILES), ALU.mult))
            with v.Fori(0, TILES // 4) as i:
                for k in range(4):
                    wait_apart(v, s["adj_in_%d" % k], (i + 1) * 16)
                    v.tensor_reduce(deg[:, ds(i * 4 + k, 1)], stage[:, k, :], AX_X, ALU.add
                                    ).then_inc(s["adj_summed"], 1)
            link = Chain(v, s["s2_chain"])
            v.wait_ge(s["adj_summed"], TILES)
            v.tensor_scalar(deg[:], deg[:], DEG_EPS, None, ALU.add).then_inc(s["rs_in"], 1)
            v.wait_ge(s["rs_out"], 2)
            rsqrt(v, link, deg[:], st[:, 2, :], dinv[:], st[:, 0, :])
            v.tensor_tensor(feat, feat, over_cols(dinv[:], TILES, 2 * P), ALU.mult).then_inc(s["setup"], 1)
            link(v.tensor_copy(v_hi, scan_v))
            link(v.tensor_tensor(v_res, scan_v, v_hi, ALU.subtract))
            link(v.tensor_copy(v_lo, v_res))
            link(v.memset(ones[:], 1.0))
            link(v.memset(xn_t[:, N:], 0.0))
            v.tensor_scalar(cols[:, 2:6], cols[:, 2:6], SCALE, None, ALU.mult).then_inc(s["scaled"], 1)
            v.memset(hc[:], 0.0).then_inc(s["scan_hc"], 1)
            v.memset(h_hi[:], 0.0).then_inc(s["scan_hi"], 1)
            v.memset(h_lo[:], 0.0).then_inc(s["scan_lo"], 1)
            v.memset(neg_one[:], -1.0).then_inc(s["setup"], 1)

            hf = cen
            link = Chain(v, s["g_chain"])
            xg = x[:, 0:AHEAD, :]
            dg = over_cols(dinv[:, 0:AHEAD], AHEAD)
            v.wait_ge(s["msg_done"], 4)
            v.tensor_copy(msg_t[:, 1, :], psum[:, 1, 0:AW]).then_inc(s["msg_v"], 1)
            v.wait_ge(s["h_done"], 1)
            for h, bank, bias in ((hf, 2, b_f), (hs_g, 3, b_s)):
                link(v.tensor_tensor(h, tiles_of(bank)[:, 0:AHEAD, :], dg, ALU.mult))
                link(v.tensor_tensor(h, h, over_rows(bias), ALU.add))
                link(v.tensor_scalar(h, h, 0.0, None, ALU.max))
            for k, h, w in ((0, hf, wa_f), (1, hs_g, wa_s)):
                link(v.tensor_tensor(wrk, h, over_rows(w), ALU.mult))
                link(v.tensor_reduce(small[:, k, 0:AHEAD], wrk, AX_X, ALU.add))
            v.tensor_tensor(small[:, 2, 0:AHEAD], small[:, 0, 0:AHEAD], small[:, 1, 0:AHEAD], ALU.add).then_inc(s["gate_in"], 1)
            link(v.tensor_tensor(hf, hf, hs_g, ALU.subtract))
            link(v.tensor_tensor(xg, xg, hs_g, ALU.add))
            v.wait_ge(s["gate_out"], 1)
            link(v.tensor_tensor(hf, hf, over_cols(small[:, 3, 0:AHEAD], AHEAD), ALU.mult))
            link(v.tensor_tensor(xg, xg, hf, ALU.add))
            centre(v, link, xg, cen, wrk, small[:, 4, 0:AHEAD], small[:, 5, 0:AHEAD], s["rs_in"])
            v.wait_ge(s["rs_out"], 3)
            rsqrt(v, link, small[:, 5, 0:AHEAD], small[:, 6, 0:AHEAD], small[:, 7, 0:AHEAD], small[:, 4, 0:AHEAD])
            v.tensor_tensor(nrm, cen, over_cols(small[:, 7, 0:AHEAD], AHEAD), ALU.mult).then_inc(s["ln_done"], 1)
            assert link.n == G_LINKS

            def norm_step(step, k, xt, col):
                total, mean, var, r, t = (s_col[:, col + c:col + c + 1] for c in range(5))
                if k == 0:
                    step(v.tensor_reduce, total, xt, AX_X, ALU.add, apart=True)
                if k == 1:
                    step(v.tensor_scalar, mean, total, 1.0 / P, None, ALU.mult)
                if k == 2:
                    step(v.tensor_scalar, s_cen, xt, mean, None, ALU.subtract)
                if k == 3:
                    step(v.tensor_tensor, s_wrk[:, 0, :], s_cen, s_cen, ALU.mult)
                if k == 4:
                    step(v.tensor_reduce, total, s_wrk[:, 0, :], AX_X, ALU.add)
                if k == 5:
                    step(v.tensor_scalar, var, total, 1.0 / P, EPS, ALU.mult, ALU.add)
                if k == 6:
                    step(v.tensor_scalar, t.bitcast(I32), var.bitcast(I32), 1, None, ALU.logical_shift_right)
                if k == 7:
                    step(v.tensor_scalar, r.bitcast(I32), t.bitcast(I32), -1.0, float(0x5f3759df), ALU.mult,
                         ALU.add)
                if 8 <= k < 17:
                    if k % 3 == 2:
                        step(v.scalar_tensor_tensor, t, r, r, var, ALU.mult, ALU.mult)
                    if k % 3 == 0:
                        step(v.tensor_scalar, t, t, -0.5, 1.5, ALU.mult, ALU.add)
                    if k % 3 == 1:
                        step(v.tensor_tensor, r, r, t, ALU.mult)
                if k == 17:
                    step(v.tensor_scalar, s_nrm, s_cen, r, None, ALU.mult)

            def graph_v(step, i, k):
                if k < 83:
                    return
                xt = x[:, ds(i + AHEAD, 1), :].rearrange("p a f -> p (a f)")
                d_col, logit, gate = (s_col[:, c:c + 1] for c in (10, 11, 5))
                if k == 83:
                    step(v.tensor_copy, d_col, dinv[:, ds(i + AHEAD, 1)])
                if k in (84, 85):
                    f = k - 84
                    if f == 0:
                        v.wait_ge(s["sg_w"], i + 1)
                    step(v.scalar_tensor_tensor, s_h[:, f, :], psum[:, 7, f * P:(f + 1) * P], d_col,
                         rows[:, f, :], ALU.mult, ALU.add)
                if k == 86:
                    step(v.tensor_scalar, s_h, s_h, 0.0, None, ALU.max)
                if k == 87:
                    step(v.tensor_tensor, s_wrk, s_h, rows[:, 2:4, :], ALU.mult)
                if k == 88:
                    step(v.tensor_reduce, logit, s_wrk.rearrange("p a f -> p (a f)"), AX_X, ALU.add)
                if k == 89:
                    step(v.tensor_tensor, s_wrk[:, 1, :], s_h[:, 0, :], s_h[:, 1, :], ALU.subtract)
                if k == 90:
                    step(v.tensor_tensor, xt, xt, s_h[:, 1, :], ALU.add)
                if k == 93:
                    v.wait_ge(s["sg_gate_out"], i + 1)
                    step(v.scalar_tensor_tensor, xt, s_wrk[:, 1, :], gate, xt, ALU.mult, ALU.add)
                norm_step(step, k - 94, xt, 0)

            def project_v(step, i, k):
                xt = x[:, ds(i, 1), :].rearrange("p a f -> p (a f)")
                if k == 4:
                    v.wait_ge(s["sp_ht"], i + 1)
                    step(v.tensor_tensor, xt, xt, psum[:, 7, 0:P], ALU.add)
                norm_step(step, k - 5, xt, 0)
                if k == 32:
                    v.wait_ge(s["sp_v"], i + 1)
                    step(v.tensor_tensor, v_nat[:, ds(i, 1), :].rearrange("p a f -> p (a f)"), psum[:, 7, 0:P],
                         b_v, ALU.add)
                h, part = (k - 38) // 5, (k - 38) % 5
                if k < 38 or h >= 2 * HEADS or part > 2:
                    return
                dst = (q_st if h < HEADS else k_st)[:, h % HEADS, ds(i * P, P)]
                src = prep_qk[:, h % 2, :]
                if part == 0:
                    v.wait_ge(s["sp_qk32"], i * 8 + (h + 1))
                    step(v.tensor_copy, dst, src)
                elif h < HEADS and part == 1:
                    step(v.tensor_tensor, dst[64:128], src[64:128], dst[64:128], ALU.subtract)
                elif h >= HEADS:
                    q = 32 if part == 1 else 96
                    step(v.tensor_tensor, dst[q:q + 32], src[q:q + 32], dst[q:q + 32], ALU.subtract)

            def beside_v(i, k, steps):
                if steps[0]:
                    graph_v(steps[0], i, k)
                if steps[1]:
                    project_v(steps[1], i - 1, k)

            def steps_of(i, graph, project):
                return (Steps(v, s["side_g"], i * SG_LINKS) if graph else None,
                        Steps(v, s["side_p"], (i - 1) * SP_LINKS) if project else None)

            def scan_v_body(i, graph, project):
                steps = steps_of(i, graph, project)
                for k in range(BODY):
                    t1 = i * BODY + (k + 1)
                    tanh_c, gates, h_k = psum[:, 4, 0:1], gates_of[:, k % 2, :], h_new[:, k:k + 1]
                    v.wait_ge(s["scan_t"], t1)
                    v.tensor_tensor(h_hi[:], gates[:, 1:2], tanh_c, ALU.mult).then_inc(s["scan_hi"], 1)
                    v.wait_ge(s["scan_hi"], t1 + 1)
                    v.scalar_tensor_tensor(h_lo[:], tanh_c, gates[:, 1:2], h_hi[:], ALU.mult, ALU.subtract
                                           ).then_inc(s["scan_lo"], 1)
                    v.scalar_tensor_tensor(cell[:], psum[:, 6, 0:1], gates[:, 0:1], hc[:],
                                           ALU.mult, ALU.add).then_inc(s["scan_c"], 1)
                    v.tensor_tensor(h_k, gates[:, 1:2], tanh_c, ALU.mult).then_inc(s["scan_h"], 1)
                    v.wait_ge(s["scan_h"], t1)
                    v.tensor_tensor(hc[:], h_k, cell[:], ALU.mult).then_inc(s["scan_hc"], 1)
                    beside_v(i, k, steps)
                v.wait_ge(s["scan_h"], (i + 1) * BODY)
                v.tensor_copy(h_prev[:], h_new[:]).then_inc(s["scan_kept"], 1)
                assert not graph or steps[0].n == SG_LINKS
                assert not project or steps[1].n == SP_LINKS

            scan_v_body(0, True, False)
            with v.Fori(1, G_BODIES) as i:
                scan_v_body(i, True, True)
            with v.Fori(G_BODIES, TILES) as i:
                scan_v_body(i, False, True)
            steps = steps_of(TILES, False, True)
            for k in range(BODY):
                beside_v(TILES, k, steps)
            v.wait_ge(s["side_p"], TILES * SP_LINKS)

            def bias_quarter(t, half, q):
                u = 2 * t + half
                c = bias_a[:, half, q * 512:(q + 1) * 512]
                v.wait_ge(s["masked"], u * 4 + q + 1)
                v.scalar_tensor_tensor(c, c, g_bias, mask[:, q % 2, :], ALU.mult, ALU.add
                                       ).then_inc(s["bias_ready"], 1)

            def evacuate_v(u, g):
                v.wait_ge(s["tp_done"], u * UT + g + 1)
                wait_past(v, s["pv_done"], u * UT, g - 3)
                v.tensor_copy(p_t[:, g % 4, :], psum[:, 4 + g % 2, :]).then_inc(s["ev_dve"], 1)

            def factors_in(t):
                link = Chain(v, s["f_chain"], t * 6)
                m0, m1 = nmx[:, 0, :], nmx[:, 1, :]
                link(v.tensor_tensor(fac[:, 0, 0:4], m0, m1, ALU.min))
                link(v.tensor_tensor(fac[:, 1, 0:4], fac[:, 0, 0:4], m0, ALU.subtract))
                v.tensor_tensor(fac[:, 1, 4:8], fac[:, 0, 0:4], m1, ALU.subtract).then_inc(s["fac_in"], 1)
                return link

            def factors_out(t, link):
                v.wait_ge(s["fac_out"], t + 1)
                link(v.tensor_tensor(fac[:, 3, :], fac[:, 2, :], lsum[:].rearrange("p a h -> p (a h)"), ALU.mult))
                link(v.tensor_tensor(fac[:, 4, 0:4], fac[:, 3, 0:4], fac[:, 3, 4:8], ALU.add))
                link(v.reciprocal(fac[:, 4, 4:8], fac[:, 4, 0:4]))
                link(v.tensor_tensor(fac[:, 5, :].rearrange("p (a h) -> p a h", a=2),
                                     fac[:, 2, :].rearrange("p (a h) -> p a h", a=2),
                                     fac[:, 4, 4:8].unsqueeze(1).to_broadcast([P, 2, HEADS]), ALU.mult))
                assert link.n == 6, link.n

            def combine(t, k):
                xt = x[:, ds(t, 1), :].rearrange("p a f -> p (a f)")
                if k:
                    v.wait_ge(s["c_chain"], t * 8 + k)
                if k == 0:
                    ins = v.tensor_tensor(xt, xt, b_out, ALU.add)
                else:
                    if k == 1:
                        v.wait_ge(s["y0_out"], t + 1)
                    if k == 5:
                        v.wait_ge(s["y_done"], 2 * t + 2)
                    h = (k - 1) % HEADS
                    y = y0[:, h * P:(h + 1) * P] if k < 5 else psum[:, 7, h * P:(h + 1) * P]
                    ins = v.scalar_tensor_tensor(xt, y, fac[:, 5, k - 1:k], xt, ALU.mult, ALU.add)
                ins.then_inc(s["c_chain" if k < 8 else "tile_done"], 1)

            def unit_v(t, half, before, after):
                u = t * 2 + half
                v.wait_ge(s["bias_ready"], (u + 1) * 4)
                for h in range(HEADS):
                    for q in range(2):
                        n = u * 8 + 2 * h + q
                        c = slice(q * PAIR, (q + 1) * PAIR)
                        if h == 0 and q == 0 and before:
                            v.wait_ge(s["tp_done"], (u - 1) * UT)
                        wait_apart(v, s["qk_done"], n + 1)
                        v.tensor_tensor_reduce(score[:, half, h, c].rearrange("p (a b) -> p a b", a=2),
                                               psum[:, 2 * q:2 * q + 2, :],
                                               bias_a[:, half, c].rearrange("p (a b) -> p a b", a=2),
                                               1.0, -3e38, ALU.add, ALU.max, mx[:, h, q:q + 1]
                                               ).then_inc(s["ttr_done"], 1)
                        if h and q == 0 and (before or half):
                            evacuate_v(u - 1, V_TILES[h - 1])
                        if h and half and before:
                            combine(t - 1, 3 * (h - 1) + q)
                    if h == 0 and half == 0 and before:
                        v.wait_ge(s["exp_done"], u * HEADS)
                        factors_out(t - 1, factors_in(t - 1))
                    v.wait_ge(s["ttr_done"], u * 8 + 2 * h + 2)
                    v.scalar_tensor_tensor(nmx[:, half, h:h + 1], mx[:, h, 0:1], mx[:, h, 1:2], neg_one[:],
                                           ALU.max, ALU.mult).then_inc(s["nm_done"], 1)
                    if after or not half:
                        for q in ((), (0,), (1,), (2, 3))[h]:
                            bias_quarter(t + half, 1 - half, q)
                    if h and half and before:
                        combine(t - 1, 3 * (h - 1) + 2)

            for q in range(4):
                bias_quarter(0, 0, q)
            for half in range(2):
                unit_v(0, half, False, True)
            with v.Fori(1, TILES - 1) as t:
                for half in range(2):
                    unit_v(t, half, True, True)
            for half in range(2):
                unit_v(TILES - 1, half, True, False)
            v.wait_ge(s["exp_done"], 2 * TILES * HEADS)
            factors_out(TILES - 1, factors_in(TILES - 1))
            for g in V_TILES:
                evacuate_v(2 * TILES - 1, g)
            for k in range(9):
                combine(TILES - 1, k)

            v.wait_ge(s["tile_done"], TILES)

            def expert_norm(j):
                link = Chain(v, s["mn_chain"], j * MN_LINKS)
                xg = x[:, ds(j * GROUP, GROUP), :]
                centre(v, link, xg, e_cen, e_wrk, small[:, 4, :], small[:, 5, :], s["m_rs_in"])
                v.wait_ge(s["m_rs_out"], j + 1)
                rsqrt(v, link, small[:, 5, :], small[:, 6, :], small[:, 7, :], small[:, 4, :])
                v.tensor_tensor(e_wrk, e_cen, over_cols(small[:, 7, :]), ALU.mult).then_inc(s["m_ln"], 1)
                assert link.n == MN_LINKS

            def experts_v(j, after):
                link = Chain(v, s["m_chain"], j * M_LINKS)
                v.wait_ge(s["m_lg"], j + 1)
                for k in range(2):
                    acc = psum[:, 1, 0:GROUP * 8].rearrange("p (t f) -> p t f", f=8)
                    link(v.tensor_tensor(lg[:], lg[:] if k else acc,
                                         gate_rows[:, k, :].unsqueeze(1).to_broadcast([P, GROUP, 8]), ALU.add),
                         k == 1)
                for k in range(GROUP):
                    link(v.max(top[:, k, :], lg[:, k, :]), True)
                    link(v.max_index(top_i[:, k, :], top[:, k, :], lg[:, k, :]), True)
                link(v.tensor_copy(top_f[:], top_i[:]))
                v.tensor_tensor(pw[:, 0, :], top[:, :, 1], top[:, :, 0], ALU.subtract).then_inc(s["m_ex_in"], 1)
                v.wait_ge(s["m_ex_out"], j + 1)
                link(v.tensor_scalar(pw[:, 0, :], pw[:, 1, :], 1.0, None, ALU.add))
                link(v.reciprocal(pw[:, 2, :], pw[:, 0, :]))
                link(v.tensor_tensor(pw[:, 3, :], pw[:, 1, :], pw[:, 2, :], ALU.mult))
                iota = gate_rows[:, 2, :].unsqueeze(1).to_broadcast([P, GROUP, 8])
                for dst, k in ((comb, 0), (comb2, 1)):
                    link(v.tensor_tensor(dst[:], iota, top_f[:, :, k:k + 1].to_broadcast([P, GROUP, 8]),
                                         ALU.is_equal))
                    link(v.tensor_tensor(dst[:], dst[:], pw[:, 2 + k, :].unsqueeze(2).to_broadcast([P, GROUP, 8]),
                                         ALU.mult))
                v.tensor_tensor(comb[:], comb[:], comb2[:], ALU.add).then_inc(s["m_comb"], 1)
                assert link.n == M_LINKS
                if after:
                    expert_norm(j + 1)
                link = Chain(v, s["e_chain"], j * E_LINKS)
                v.wait_ge(s["m_comb"], j + 1)
                for k in range(GROUP):
                    xt = x[:, ds(j * GROUP + k, 1), :].rearrange("p a f -> p (a f)")
                    for b in range(3):
                        n = k * 3 + b
                        v.wait_ge(s["e_y"], j * 12 + (n + 1))
                        bank = psum[:, 5 + n % 3, :]
                        for q in range(4 if b < 2 else 1):
                            y = bank[:, q * P:(q + 1) * P]
                            last = b == 2 or q == 3
                            if b < 2:
                                w = comb[:, k, b * 4 + q:b * 4 + q + 1]
                                ins = v.scalar_tensor_tensor(xt, y, w, xt, ALU.mult, ALU.add)
                            else:
                                ins = v.tensor_tensor(xt, xt, y, ALU.add)
                            if last:
                                ins.then_inc(s["e_used"], 1)
                                v.wait_ge(s["e_used"], j * 12 + (n + 1))
                            else:
                                link(ins)
                assert link.n == E_LINKS

            expert_norm(0)
            with v.Fori(0, GROUPS - 1) as j:
                experts_v(j, True)
            experts_v(GROUPS - 1, False)

        @block.gpsimd
        def _(g):
            def mask_unit(t, half):
                for q in range(4):
                    n = 4 * half + q
                    if q == 0:
                        wait_apart(g, s["bias_in_%d" % half], (t + 1) * 16)
                    if isinstance(t, int) and t == 0:
                        if n > 1:
                            g.wait_ge(s["bias_ready"], n - 1)
                    else:
                        wait_apart(g, s["bias_ready"], t * 8 + (n - 1))
                    g.tensor_scalar(mask[:, q % 2, :], bias_a[:, half, q * 512:(q + 1) * 512], 0.0, MASKED,
                                    ALU.is_equal, ALU.mult).then_inc(s["masked"], 1)

            g.wait_ge(s["setup"], 2)
            for half in range(2):
                mask_unit(0, half)
            with g.Fori(1, TILES) as t:
                for half in range(2):
                    mask_unit(t, half)

        @block.scalar
        def _(a):
            a.wait_ge(s["rs_in"], 1)
            a.activation(st[:, 2, :], st[:, 1, :], ACT.Sqrt).then_inc(s["rs_out"], 1)
            a.wait_ge(s["rs_in"], 2)
            a.activation(st[:, 2, :], deg[:], ACT.Sqrt).then_inc(s["rs_out"], 1)
            a.wait_ge(s["msg_done"], 4)
            a.activation(msg_t[:, 0, :], psum[:, 0, 0:AW], ACT.Copy).then_inc(s["msg_a"], 1)
            a.wait_ge(s["gate_in"], 1)
            a.activation(small[:, 3, 0:AHEAD], small[:, 2, 0:AHEAD], ACT.Sigmoid, bias=b_att).then_inc(s["gate_out"], 1)
            a.wait_ge(s["rs_in"], 3)
            a.activation(small[:, 6, 0:AHEAD], small[:, 5, 0:AHEAD], ACT.Sqrt).then_inc(s["rs_out"], 1)
            a.wait_ge(s["xt_done"], 1)
            a.activation(xn_t[:, 0:AW], psum[:, 4, 0:AW], ACT.Copy).then_inc(s["xt_out"], 1)

            def graph_a(i, k):
                if k == 66:
                    a.wait_ge(s["sg_msg"], i + 1)
                    a.activation(s_msg_t.rearrange("p a f -> p (a f)"), psum[:, 5, 0:2 * P], ACT.Copy
                                 ).then_inc(s["sg_msg_t"], 1)
                if k == 91:
                    a.wait_ge(s["side_g"], i * SG_LINKS + SG_LOGIT)
                    a.activation(s_col[:, 5:6], s_col[:, 11:12], ACT.Sigmoid, bias=b_att
                                 ).then_inc(s["sg_gate_out"], 1)
                if k == 117:
                    a.wait_ge(s["sg_xt"], i + 1)
                    a.activation(xn_t[:, ds((i + AHEAD) * P, P)], psum[:, 7, 0:P], ACT.Copy
                                 ).then_inc(s["sg_xt_out"], 1)

            def project_a(i, k):
                if k == 27:
                    a.wait_ge(s["sp_xt"], i + 1)
                    a.activation(prep_t, psum[:, 7, 0:P], ACT.Copy).then_inc(s["sp_xt_out"], 1)
                h = (k - 36) // 5
                if k >= 36 and (k - 36) % 5 == 0 and h < 2 * HEADS:
                    a.wait_ge(s["sp_qk"], i * 8 + (h + 1))
                    if h >= 2:
                        split = SP_V + sum(2 if g < HEADS else 3 for g in range(h - 1))
                        a.wait_ge(s["side_p"], i * SP_LINKS + split)
                    a.activation(prep_qk[:, h % 2, :], psum[:, 7, 0:P], ACT.Identity,
                                 bias=cols[:, 2 + h:3 + h], scale=SCALE if h < HEADS else 1.0
                                 ).then_inc(s["sp_qk32"], 1)

            a.wait_ge(s["setup"], 2)
            a.wait_ge(s["scaled"], 1)

            def scan_a_body(i, graph, project):
                a.activation(tables[:], neg_one[:], ACT.Sigmoid)
                for k in range(BODY):
                    t1 = i * BODY + (k + 1)
                    gates = gates_of[:, k % 2, :]
                    gate_g = psum[:, 6, 0:1]
                    bank = k // STEPS % 2
                    c = k % STEPS
                    a.wait_ge(s["scan_zg"], t1)
                    if k or not isinstance(i, int):
                        a.wait_ge(s["scan_c"], i * BODY + k)
                    a.activation(gate_g, psum[:, 2 + bank, c:c + 1], ACT.Tanh)
                    a.wait_ge(s["scan_z"], t1)
                    a.activation(gates, psum[:, bank, c:c + STEPS + 1:STEPS], ACT.Sigmoid).then_inc(s["scan_io"], 1)
                    a.wait_ge(s["scan_io"], t1)
                    a.wait_ge(s["scan_hc"], t1)
                    a.activation(psum[:, 4, 0:1], gate_g, ACT.Tanh, bias=hc[:, 0:1], scale=gates[:, 0:1]
                                 ).then_inc(s["scan_t"], 1)

                    if graph:
                        graph_a(i, k)
                    if project:
                        project_a(i - 1, k)

            scan_a_body(0, True, False)
            with a.Fori(1, G_BODIES) as i:
                scan_a_body(i, True, True)
            with a.Fori(G_BODIES, TILES) as i:
                scan_a_body(i, False, True)
            for k in range(BODY):
                project_a(TILES - 1, k)

            def evacuate_a(u, g):
                a.wait_ge(s["tp_done"], u * UT + g + 1)
                wait_past(a, s["pv_done"], u * UT, g - 3)
                a.activation(p_t[:, g % 4, :], psum[:, 4 + g % 2, :], ACT.Copy).then_inc(s["ev_act"], 1)

            def exponent(u, half, h):
                a.wait_ge(s["nm_done"], u * HEADS + h + 1)
                sc = score[:, half, h, :]
                a.activation(sc, sc, ACT.Exp, bias=nmx[:, half, h:h + 1], accum_out=lsum[:, half, h:h + 1]
                             ).then_inc(s["exp_done"], 1)

            def outputs_a(u):
                a.wait_ge(s["pv_done"], (u + 1) * UT)
                wait_past(a, s["y_done"], u, 0)
                a.activation(o_t[:], psum[:, 6, 0:P], ACT.Copy).then_inc(s["o_out"], 1)

            def keep_y0(u, t):
                wait_past(a, s["tile_done"], t, 0)
                a.wait_ge(s["y_done"], u + 1)
                a.activation(y0[:], psum[:, 7, :], ACT.Copy).then_inc(s["y0_out"], 1)

            def factors_a(t):
                a.wait_ge(s["fac_in"], t + 1)
                a.activation(fac[:, 2, :], fac[:, 1, :], ACT.Exp).then_inc(s["fac_out"], 1)

            def first_slot_a(t, half, done):
                u = t * 2 + half
                exponent(u - 1, 1 - half, HEADS - 1)
                if done:
                    outputs_a(u - 2)
                for g in (0, 1):
                    evacuate_a(u - 1, g)
                if half == 0:
                    factors_a(t - 1)
                if half == 0 and done:
                    keep_y0(u - 2, t - 1)
                for g in (2, 3):
                    evacuate_a(u - 1, g)

            def unit_a(t, half, before):
                u = t * 2 + half
                if before or half:
                    first_slot_a(t, half, before)
                for h in range(1, HEADS):
                    exponent(u, half, h - 1)
                    if before or half:
                        for g in range(4 * h, 4 * h + 4):
                            if g not in V_TILES:
                                evacuate_a(u - 1, g)

            for half in range(2):
                unit_a(0, half, False)
            with a.Fori(1, TILES) as t:
                for half in range(2):
                    unit_a(t, half, True)
            first_slot_a(TILES, 0, True)
            for g in range(4, UT):
                if g not in V_TILES:
                    evacuate_a(2 * TILES - 1, g)
            outputs_a(2 * TILES - 1)

            def expert_root(j):
                a.wait_ge(s["m_rs_in"], j + 1)
                a.activation(small[:, 6, :], small[:, 5, :], ACT.Sqrt).then_inc(s["m_rs_out"], 1)

            def expert_rows(j):
                a.wait_ge(s["m_xt"], j + 1)
                a.activation(xe_t, psum[:, 0, :], ACT.Copy).then_inc(s["m_xt_out"], 1)

            def experts_a(j, after):
                a.wait_ge(s["m_ex_in"], j + 1)
                a.activation(pw[:, 1, :], pw[:, 0, :], ACT.Exp).then_inc(s["m_ex_out"], 1)
                for k in range(HT):
                    a.wait_ge(s["e_h"], j * HT + k + 1)
                    a.activation(hid_t[:, k, :], psum[:, 2 + k % 3, :], ACT.Relu, bias=e_b1[:, k:k + 1]
                                 ).then_inc(s["e_hid"], 1)
                    if after and k == HT // 2:
                        expert_root(j + 1)
                a.wait_ge(s["m_ct"], j + 1)
                a.activation(comb_t[:], psum[0:EXPERTS, 1, :], ACT.Copy).then_inc(s["m_ct_out"], 1)
                if after:
                    expert_rows(j + 1)

            expert_root(0)
            expert_rows(0)
            with a.Fori(0, GROUPS - 1) as j:
                experts_a(j, True)
            experts_a(GROUPS - 1, False)

        @block.tensor
        def _(pe):
            pe.wait_ge(s["consts_in"], 16 * len(consts))
            pe.wait_ge(s["setup"], 1)
            for k in range(4):
                pe.wait_ge(s["adj_t_in_%d" % k], 16)
                for b in range(8):
                    m = 8 * k + b
                    for f in range(2):
                        mm = pe.matmul(psum[:, f, 0:AW], feat[:, m, f * P:(f + 1) * P],
                                       first_adj[k][:, b * AW:(b + 1) * AW], start=(m == 0), stop=(m == TILES - 1))
                mm.then_inc(s["msg_done"], 1)
            pe.wait_ge(s["msg_a"], 1)
            pe.wait_ge(s["msg_v"], 1)
            for f in range(2):
                for t in range(AHEAD):
                    mm = pe.matmul(psum[:, 2 + f, t * P:(t + 1) * P], msg_t[:, f, t * P:(t + 1) * P],
                                   gcn_w[:, f, :], start=True, stop=True)
            mm.then_inc(s["h_done"], 1)
            pe.wait_ge(s["ln_done"], 1)
            for t in range(AHEAD):
                mm = pe.transpose(psum[:, 4, t * P:(t + 1) * P], nrm[:, t, :], ident[:])
            mm.then_inc(s["xt_done"], 1)

            def graph_pe(i, k):
                if k < 2 * TILES:
                    if k == 0:
                        pe.wait_ge(s["sg_adj_in"], (i + 1) * 16)
                    m, f = k // 2, k % 2
                    mm = pe.matmul(psum[:, 5, f * P:(f + 1) * P], feat[:, m, f * P:(f + 1) * P],
                                   stage_s[:, m * P:(m + 1) * P], start=(k == 0), stop=(m == TILES - 1),
                                   skip_group_check=True)
                    if k == 2 * TILES - 1:
                        mm.then_inc(s["sg_msg"], 1)
                if k in (73, 74):
                    f = k - 73
                    if f == 0:
                        if not isinstance(i, int):
                            pe.wait_ge(s["sp_qk32"], i * 8)
                        pe.wait_ge(s["sg_msg_t"], i + 1)
                    mm = pe.matmul(psum[:, 7, f * P:(f + 1) * P], s_msg_t[:, f, :], gcn_w[:, f, :],
                                   start=True, stop=True)
                    if f:
                        mm.then_inc(s["sg_w"], 1)
                if k == 115:
                    pe.wait_ge(s["side_g"], (i + 1) * SG_LINKS)
                    if not isinstance(i, int):
                        pe.wait_ge(s["sg_xt_out"], i)
                    pe.transpose(psum[:, 7, 0:P], s_nrm, ident[:]).then_inc(s["sg_xt"], 1)

            def project_pe(i, k, i_graph):
                if k == 1:
                    pe.wait_ge(s["scan_kept"], i + 1)
                    if i_graph is not None:
                        pe.wait_ge(s["sg_xt_out"], i_graph)
                    pe.transpose(psum[:, 7, 0:P], h_prev[:], ident[:]).then_inc(s["sp_ht"], 1)
                if k == 25:
                    pe.wait_ge(s["side_p"], i * SP_LINKS + (SP_V - 1))
                    pe.transpose(psum[:, 7, 0:P], s_nrm, ident[:]).then_inc(s["sp_xt"], 1)
                if k == 29:
                    pe.wait_ge(s["sp_xt_out"], i + 1)
                    pe.matmul(psum[:, 7, 0:P], prep_t, prep_w[:, 2 * HEADS, :], start=True, stop=True
                              ).then_inc(s["sp_v"], 1)
                h = (k - 34) // 5
                if k >= 34 and (k - 34) % 5 == 0 and h < 2 * HEADS:
                    if h == 0:
                        pe.wait_ge(s["side_p"], i * SP_LINKS + SP_V)
                    else:
                        pe.wait_ge(s["sp_qk32"], i * 8 + h)
                    pe.matmul(psum[:, 7, 0:P], prep_w[:, h, :], prep_t, start=True, stop=True
                              ).then_inc(s["sp_qk"], 1)

            def gate_sums(bank, g):
                return psum[:, bank, g * STEPS:(g + 1) * STEPS] if g < 2 else psum[:, 2 + bank, 0:STEPS]

            def inputs_of(bank, at, k):
                g = k // 2
                dst = gate_sums(bank, g)
                if k % 2 == 0:
                    pe.matmul(dst, scan_u[:, g, :], xn_t[:, ds(at, STEPS)], start=(g != 1), stop=False,
                              skip_group_check=True)
                else:
                    pe.matmul(dst, scan_b[:, g, :], ones[:], start=False, stop=False, skip_group_check=True)

            pe.wait_ge(s["setup"], 2)
            pe.wait_ge(s["xt_out"], 1)
            pe.wait_ge(s["prepw_in"], 16)
            for k in range(6):
                inputs_of(0, 0, k)

            def scan_pe_body(i, graph, project):
                for k in range(BODY):
                    b, c = k // STEPS % 2, k % STEPS
                    acc = [gate_sums(b, g)[:, c:c + 1] for g in range(3)]
                    pe.wait_ge(s["scan_hi"], i * BODY + (k + 1))
                    for part in (v_lo, v_hi):
                        for g in range(3):
                            pe.matmul(acc[g], part[:, g, :], h_hi[:], start=False, stop=False,
                                      skip_group_check=True)
                    pe.wait_ge(s["scan_lo"], i * BODY + (k + 1))
                    for g, signal in ((2, "scan_zg"), (0, None), (1, "scan_z")):
                        mm = pe.matmul(acc[g], v_hi[:, g, :], h_lo[:], start=False, stop=False,
                                       skip_group_check=True)
                        if signal:
                            mm.then_inc(s[signal], 1)
                    if c < 6:
                        inputs_of(1 - b, i * BODY + (k // STEPS + 1) * STEPS, c)

                    if graph:
                        graph_pe(i, k)
                    if project:
                        project_pe(i - 1, k, i if graph else None)

            scan_pe_body(0, True, False)
            with pe.Fori(1, G_BODIES) as i:
                scan_pe_body(i, True, True)
            pe.wait_ge(s["sg_xt_out"], G_BODIES)
            with pe.Fori(G_BODIES, TILES) as i:
                scan_pe_body(i, False, True)
            for k in range(BODY):
                project_pe(TILES - 1, k, None)

            def scores(u, t, half, h, q):
                n = 8 * half + 2 * h + q
                wait_past(pe, s["ttr_done"], t * 16, n - 1)
                for c in range(2):
                    at = half * HALF + q * PAIR + c * 512
                    mm = pe.matmul(psum[:, 2 * q + c, :], q_st[:, h, ds(t * P, P)], k_st[:, h, at:at + 512],
                                   start=True, stop=True)
                mm.then_inc(s["qk_done"], 1)

            def transposes(u, half, g):
                if g == 0:
                    pe.wait_ge(s["exp_done"], (u + 1) * HEADS)
                if g >= 2:
                    wait_evacuated(pe, u, g - 2)
                elif not isinstance(u, int) or u > 0:
                    wait_evacuated(pe, u - 1, UT + g - 2)
                for h in range(HEADS):
                    mm = pe.transpose(psum[:, 4 + g % 2, h * P:(h + 1) * P],
                                      score[:, half, h, g * P:(g + 1) * P], ident[:])
                mm.then_inc(s["tp_done"], 1)

            def values(u, half, g):
                if g == 0:
                    wait_past(pe, s["o_out"], u, 0)
                wait_evacuated(pe, u, g)
                for h in range(HEADS):
                    mm = pe.matmul(psum[h * HD:(h + 1) * HD, 6, 0:P],
                                   v_nat[:, half * UT + g, h * HD:(h + 1) * HD],
                                   p_t[:, g % 4, h * P:(h + 1) * P], start=(g == 0), stop=(g == UT - 1),
                                   skip_group_check=True)
                mm.then_inc(s["pv_done"], 1)

            def project(u, t, half):
                pe.wait_ge(s["o_out"], u + 1)
                if half:
                    pe.wait_ge(s["y0_out"], t + 1)
                else:
                    wait_past(pe, s["tile_done"], t, 0)
                pe.matmul(psum[:, 7, :], o_t[:], w_out[:], start=True, stop=True).then_inc(s["y_done"], 1)

            def column(u, half, g):
                transposes(u, half, g)
                if g >= 2:
                    values(u, half, g - 2)

            def unit_pe(t, half, before, after):
                u = t * 2 + half
                w, w_half = u - 1, 1 - half
                for h in range(HEADS):
                    nxt = (u, t, half, h + 1)
                    if h == HEADS - 1:
                        nxt = (u + 1, t + half, 1 - half, 0)
                    last = h == HEADS - 1 and half and not after
                    if h == 0 and before:
                        values(u - 2, half, UT - 2)
                        values(u - 2, half, UT - 1)
                    if before or half:
                        column(w, w_half, 4 * h)
                        if h:
                            column(w, w_half, 4 * h + 1)
                    if not last:
                        scores(*nxt, 0)
                    if before or half:
                        column(w, w_half, 4 * h + (2 if h else 1))
                    if h == 0 and before:
                        project(u - 2, t - 1, half)
                    if h == 0 and (before or half):
                        column(w, w_half, 2)
                    if before or half:
                        column(w, w_half, 4 * h + 3)
                    if not last:
                        scores(*nxt, 1)

            pe.wait_ge(s["side_p"], TILES * SP_LINKS)
            for q in range(2):
                scores(0, 0, 0, 0, q)
            for half in range(2):
                unit_pe(0, half, False, True)
            with pe.Fori(1, TILES - 1) as t:
                for half in range(2):
                    unit_pe(t, half, True, True)
            for half in range(2):
                unit_pe(TILES - 1, half, True, False)
            last = 2 * TILES - 1
            values(last - 1, 0, UT - 2)
            values(last - 1, 0, UT - 1)
            column(last, 1, 0)
            column(last, 1, 1)
            project(last - 1, TILES - 1, 0)
            for g in range(2, UT):
                column(last, 1, g)
            values(last, 1, UT - 2)
            values(last, 1, UT - 1)
            project(last, TILES - 1, 1)

            pe.wait_ge(s["expw_in"], 32)

            def expert_rows_t(j):
                pe.wait_ge(s["m_ln"], j + 1)
                for t in range(GROUP):
                    mm = pe.transpose(psum[:, 0, t * P:(t + 1) * P], e_wrk[:, t, :], ident[:])
                mm.then_inc(s["m_xt"], 1)

            def gate_logits(j):
                pe.wait_ge(s["m_xt_out"], j + 1)
                for t in range(GROUP):
                    mm = pe.matmul(psum[:, 1, t * EXPERTS:(t + 1) * EXPERTS], xe_t[:, t * P:(t + 1) * P],
                                   e_wg[:], start=True, stop=True)
                mm.then_inc(s["m_lg"], 1)

            def experts_pe(j, after):
                for k in range(HT):
                    if k > 2:
                        pe.wait_ge(s["e_hid"], j * HT + (k - 2))
                    pe.matmul(psum[:, 2 + k % 3, :], e_w1[:, k * P:(k + 1) * P], xe_t,
                              start=True, stop=True).then_inc(s["e_h"], 1)
                pe.wait_ge(s["m_comb"], j + 1)
                for t in range(GROUP):
                    mm = pe.transpose(psum[0:EXPERTS, 1, t * P:(t + 1) * P], comb[:, t, :], ident[:])
                mm.then_inc(s["m_ct"], 1)
                if after:
                    expert_rows_t(j + 1)
                pe.wait_ge(s["e_hid"], (j + 1) * HT)
                pe.wait_ge(s["m_ct_out"], j + 1)
                for k in range(GROUP):
                    rows_k = slice(k * P, (k + 1) * P)
                    for b in range(3):
                        n = k * 3 + b
                        if n > 2:
                            pe.wait_ge(s["e_used"], j * 3 * GROUP + (n - 2))
                        if b == 2:
                            mm = pe.matmul(psum[:, 5 + n % 3, 0:P], comb_t[:, rows_k], e_b2[:],
                                           start=True, stop=True)
                        else:
                            for q in range(4):
                                for i in range(2):
                                    m = 2 * (4 * b + q) + i
                                    mm = pe.matmul(psum[:, 5 + n % 3, q * P:(q + 1) * P], hid_t[:, m, rows_k],
                                                   e_w2[:, m, :], start=(i == 0), stop=(i == 1))
                        mm.then_inc(s["e_y"], 1)
                    if k == 0 and after:
                        gate_logits(j + 1)

            expert_rows_t(0)
            gate_logits(0)
            with pe.Fori(0, GROUPS - 1) as j:
                experts_pe(j, True)
            experts_pe(GROUPS - 1, False)


def kernel(x, adj, L0_gnn_spatial_x, L0_gnn_W_f, L0_gnn_b_f, L0_gnn_W_s, L0_gnn_b_s, L0_gnn_W_att,
           L0_gnn_b_att, L0_ffn_U_i, L0_ffn_V_i, L0_ffn_b_i, L0_ffn_U_f, L0_ffn_V_f, L0_ffn_b_f,
           L0_ffn_U_c, L0_ffn_V_c, L0_ffn_b_c, L0_ffn_U_o, L0_ffn_V_o, L0_ffn_b_o, L1_gnn_Wqkv,
           L1_gnn_bqkv, L1_gnn_Wout, L1_gnn_bout, L1_gnn_graph_bias, L1_ffn_Wg, L1_ffn_bg,
           L1_ffn_bias, L1_ffn_W1, L1_ffn_b1, L1_ffn_W2, L1_ffn_b2):
    import concourse.bacc as bacc
    from concourse.bass_utils import run_bass_kernel_spmd

    def on_rows(v):
        return np.broadcast_to(np.asarray(v).reshape(1, -1), (P, v.size))

    def per_head(w):
        return [np.tile(w[..., h * HD:(h + 1) * HD], 4) for h in range(HEADS)]

    x, adj, wqkv, bqkv = (np.asarray(v) for v in (x, adj, L1_gnn_Wqkv, L1_gnn_bqkv))
    w_att, w_o = np.asarray(L0_gnn_W_att), np.asarray(L1_gnn_Wout)
    w_out = np.zeros((P, HEADS, P), np.float32)
    for h in range(HEADS):
        w_out[h * HD:(h + 1) * HD, h] = w_o[h * HD:(h + 1) * HD]
    arrays = {
        "x": x, "spatial": np.asarray(L0_gnn_spatial_x), "adj": adj, "adj_t": np.ascontiguousarray(adj.T),
        "ident": np.eye(P, dtype=np.float32),
        "rows": np.stack([on_rows(v) for v in (L0_gnn_b_f, L0_gnn_b_s, w_att[:P], w_att[P:], L1_gnn_bout,
                                               bqkv[2 * P:])], 1),
        "gcn_w": np.stack([L0_gnn_W_f, L0_gnn_W_s], 1),
        "cols": np.concatenate([on_rows(np.asarray(L0_gnn_b_att)), on_rows(np.asarray(L1_gnn_graph_bias)),
                                np.stack(per_head(bqkv[:P]) + per_head(bqkv[P:2 * P]), 1)], 1),
        "gate_rows": np.stack([on_rows(np.asarray(v)) for v in (L1_ffn_bg, L1_ffn_bias,
                                                                np.arange(EXPERTS, dtype=np.float32))], 1),
        "scan_v": np.stack([L0_ffn_V_i, L0_ffn_V_o, L0_ffn_V_c], 1),
        "scan_u": np.stack([L0_ffn_U_i, L0_ffn_U_o, L0_ffn_U_c], 1),
        "scan_b": np.stack([L0_ffn_b_i, L0_ffn_b_o, L0_ffn_b_c])[None],
        "w_out": w_out.reshape(P, HEADS * P),
        "qkv_w": np.stack(per_head(wqkv[:, :P]) + per_head(wqkv[:, P:2 * P]) + [wqkv[:, 2 * P:]], 1),
        "e_w1": np.transpose(L1_ffn_W1, (1, 0, 2)).reshape(P, EXPERTS * HID),
        "e_w2": np.transpose(np.asarray(L1_ffn_W2).reshape(HT, P, P), (1, 0, 2)),
        "e_b1": np.asarray(L1_ffn_b1).reshape(HT, P).T,
        "e_b2": np.asarray(L1_ffn_b2),
        "e_wg": np.asarray(L1_ffn_Wg),
    }
    arrays = {k: np.ascontiguousarray(v) for k, v in arrays.items()}
    nc = bacc.Bacc("TRN2", target_bir_lowering=False, num_devices=1)
    d = {k: nc.dram_tensor("in_" + k, v.shape, F32, kind="ExternalInput").ap() for k, v in arrays.items()}
    out = nc.dram_tensor("out", (N, P), F32, kind="ExternalOutput").ap()
    build(nc, d, out)
    return run_bass_kernel_spmd(nc, [{"in_" + k: v for k, v in arrays.items()}], core_ids=[0]).results[0]["out"]
```
